# Optimizing a Trainium2 kernel written in Bass

```python
import numpy as np
import jax
import jax.numpy as jnp

def _softmax(x, axis=-1):
    return jax.nn.softmax(x, axis=axis)

def _gelu(x):
    return jax.nn.gelu(x, approximate=True)

def _silu(x):
    return jax.nn.silu(x)

def _sigmoid(x):
    return jax.nn.sigmoid(x)

def _layernorm(x, axis=-1, eps=1e-05):
    m = jnp.mean(x, axis=axis, keepdims=True)
    v = jnp.var(x, axis=axis, keepdims=True)
    return (x - m) / jnp.sqrt(v + eps)

def _scatter_add(tgt, idx, src, axis=0):
    return tgt.at[idx].add(src)

def _segment_sum(src, seg, n):
    return jax.ops.segment_sum(src, seg, n)
kernel_name = 'mk_flamingo_gated_d1_seqx_r8_b3f39c'

def setup_inputs(seed: int=0):
    np.random.seed(seed)
    _w = jnp.asarray

    def _rec_inputs():
        import jax
        import jax.numpy as jnp
        _rk = jax.random.key(seed)
        x = 0.0003765 + 1 * jax.random.normal(jax.random.fold_in(_rk, 1), (16, 128, 256), jnp.float32)
        _lenS = 128 - jax.random.randint(jax.random.fold_in(_rk, 7), (16,), 0, max(1, 128 // 4) + 1, jnp.int32)
        _lenS2 = 128 - jax.random.randint(jax.random.fold_in(_rk, 8), (16,), 0, max(1, 128 // 4) + 1, jnp.int32)
        _ctx_2048P = jax.random.normal(jax.random.fold_in(_rk, 11), (16, 16, 256), jnp.float32)
        _ctx_2048c = jax.random.dirichlet(jax.random.fold_in(_rk, 511), 0.3 * jnp.ones((16,), jnp.float32), (16, 128))
        _ctx_2048t = jnp.einsum('bsk,bkd->bsd', _ctx_2048c, _ctx_2048P)
        _ctx_2048t = _ctx_2048t * jax.lax.rsqrt(jnp.mean(jnp.square(_ctx_2048t)) + 1e-12) * 0.953939
        ctx_2048 = -0.000292821 + 1.00034 * (_ctx_2048t + 0.3 * jax.random.normal(jax.random.fold_in(_rk, 611), (16, 128, 256), jnp.float32))
        _g = jax.random.normal(jax.random.fold_in(_rk, 9001), (2, 1), jnp.float32)
        _g = jnp.sign(_g) * jnp.maximum(jnp.abs(_g), 1.0) + (_g == 0) * 1.0
        g_xattn = _g[0]
        g_ffn = _g[1]
        return (x, ctx_2048, g_xattn, g_ffn)
    x, ctx_2048, g_xattn, g_ffn = _rec_inputs()

    def _L0_xattn_setup():
        import jax, jax.numpy as jnp
        import numpy as np
        key = jax.random.key(seed)
        k1, k2, k3, k4, k5 = jax.random.split(key, 5)
        B, D_MODEL, L = (2, 128, 256)
        HEAD_DIM = 8
        H = D_MODEL // HEAD_DIM
        return {'k': jax.random.normal(k1, (B, D_MODEL, L), dtype=jnp.float32), 'v': jax.random.normal(k2, (B, D_MODEL, L), dtype=jnp.float32), 'q': jax.random.normal(k3, (B, D_MODEL, L), dtype=jnp.float32), 'ssm_kernel': jax.random.normal(k4, (H, L), dtype=jnp.float32), 'D': jax.random.normal(k5, (H,), dtype=jnp.float32), 'head_dim': HEAD_DIM}
    _L0_xattn_all = _L0_xattn_setup()
    _L0_xattn_in = {k: v for k, v in _L0_xattn_all.items() if k in ('ssm_kernel', 'D')}
    del _L0_xattn_all

    def _L0_ffn_setup():
        import jax, jax.numpy as jnp
        import numpy as np
        H = 256
        M = 176
        E = 32
        TOPK = 6
        G = 8
        TOPK_G = 4
        SH = 2
        B, S = (1, 128)
        key = jax.random.key(seed)
        ks = jax.random.split(key, 9)
        sc = 0.02
        return {'x': jax.random.normal(ks[0], (B, S, H), dtype=jnp.float32), 'w_router': jax.random.normal(ks[1], (H, E), dtype=jnp.float32) * sc, 'corr_bias': jax.random.normal(ks[2], (E,), dtype=jnp.float32) * 0.1, 'gate_w': jax.random.normal(ks[3], (E, H, M), dtype=jnp.float32) * sc, 'up_w': jax.random.normal(ks[4], (E, H, M), dtype=jnp.float32) * sc, 'down_w': jax.random.normal(ks[5], (E, M, H), dtype=jnp.float32) * sc, 'sh_gate_w': jax.random.normal(ks[6], (H, M * SH), dtype=jnp.float32) * sc, 'sh_up_w': jax.random.normal(ks[7], (H, M * SH), dtype=jnp.float32) * sc, 'sh_down_w': jax.random.normal(ks[8], (M * SH, H), dtype=jnp.float32) * sc}
    _L0_ffn_all = _L0_ffn_setup()
    _L0_ffn_in = {k: v for k, v in _L0_ffn_all.items() if k in ('w_router', 'corr_bias', 'gate_w', 'up_w', 'down_w', 'sh_gate_w', 'sh_up_w', 'sh_down_w')}
    del _L0_ffn_all
    return {'x': x, 'ctx_2048': ctx_2048, 'g_xattn': g_xattn, 'g_ffn': g_ffn, 'L0_xattn_ssm_kernel': _L0_xattn_in['ssm_kernel'], 'L0_xattn_D': _L0_xattn_in['D'], 'L0_ffn_w_router': _L0_ffn_in['w_router'], 'L0_ffn_corr_bias': _L0_ffn_in['corr_bias'], 'L0_ffn_gate_w': _L0_ffn_in['gate_w'], 'L0_ffn_up_w': _L0_ffn_in['up_w'], 'L0_ffn_down_w': _L0_ffn_in['down_w'], 'L0_ffn_sh_gate_w': _L0_ffn_in['sh_gate_w'], 'L0_ffn_sh_up_w': _L0_ffn_in['sh_up_w'], 'L0_ffn_sh_down_w': _L0_ffn_in['sh_down_w']}

def reference(x, ctx_2048, g_xattn, g_ffn, L0_xattn_ssm_kernel, L0_xattn_D, L0_ffn_w_router, L0_ffn_corr_bias, L0_ffn_gate_w, L0_ffn_up_w, L0_ffn_down_w, L0_ffn_sh_gate_w, L0_ffn_sh_up_w, L0_ffn_sh_down_w):
    import jax
    import jax.numpy as jnp

    def _L0_xattn_ref(k, v, q, ssm_kernel, D, head_dim):
        import jax, jax.numpy as jnp
        import numpy as np
        B, HD, L = k.shape
        H = HD // head_dim
        fft_size = 2 * L
        k_ = k.reshape(B, H, head_dim, L)
        v_ = v.reshape(B, H, head_dim, L)
        q_ = q.reshape(B, H, head_dim, L)
        kv = jnp.einsum('bhil,bhjl->bijhl', k_, v_)
        kv_f = jnp.fft.rfft(kv, n=fft_size)
        kernel_f = jnp.fft.rfft(ssm_kernel, n=fft_size)
        y = jnp.fft.irfft(kv_f * kernel_f, n=fft_size)[..., :L]
        out = y + kv * D[None, None, None, :, None]
        out = jnp.einsum('bijhl,bhil->bjhl', out, q_)
        out = jnp.transpose(out, (0, 2, 1, 3)).reshape(B, H * head_dim, L)
        return out.astype(k.dtype)

    def _L0_ffn_ref(x, w_router, corr_bias, gate_w, up_w, down_w, sh_gate_w, sh_up_w, sh_down_w):
        import jax, jax.numpy as jnp
        import numpy as np
        H = 256
        M = 176
        E = 32
        TOPK = 6
        G = 8
        TOPK_G = 4
        SH = 2
        B, S = (1, 128)
        b, s, h = x.shape
        xf = x.reshape(-1, h)
        T = xf.shape[0]
        logits = xf @ w_router
        scores = jax.nn.sigmoid(logits)
        sfc = scores + corr_bias
        grp = sfc.reshape(T, G, E // G)
        top2, _ = jax.lax.top_k(grp, 2)
        group_scores = top2.sum(-1)
        _, gidx = jax.lax.top_k(group_scores, TOPK_G)
        group_mask = jax.nn.one_hot(gidx, G, dtype=jnp.float32).sum(axis=1) > 0
        score_mask = jnp.repeat(group_mask, E // G, axis=1)
        masked = jnp.where(score_mask, sfc, -jnp.inf)
        _, topk_idx = jax.lax.top_k(masked, TOPK)
        topk_w = jnp.take_along_axis(scores, topk_idx, axis=1)
        combine = jnp.zeros((T, E), dtype=x.dtype).at[jnp.arange(T)[:, None], topk_idx].add(topk_w)
        g = jnp.einsum('th,ehm->etm', xf, gate_w)
        u = jnp.einsum('th,ehm->etm', xf, up_w)
        eo = jnp.einsum('etm,emh->eth', jax.nn.silu(g) * u, down_w)
        routed = jnp.einsum('te,eth->th', combine, eo)
        shared = jax.nn.silu(xf @ sh_gate_w) * (xf @ sh_up_w) @ sh_down_w
        return (routed + shared).reshape(b, s, h)
    x = x + jnp.tanh(g_xattn[0]) * _L0_xattn_ref(ctx_2048, ctx_2048, _layernorm(x, axis=-1), L0_xattn_ssm_kernel, L0_xattn_D, 8)
    x = x + jnp.tanh(g_ffn[0]) * _L0_ffn_ref(_layernorm(x, axis=-1), L0_ffn_w_router, L0_ffn_corr_bias, L0_ffn_gate_w, L0_ffn_up_w, L0_ffn_down_w, L0_ffn_sh_gate_w, L0_ffn_sh_up_w, L0_ffn_sh_down_w)
    return x

_drawn_inputs = setup_inputs


def setup_inputs(seed=0):
    import zlib

    import numpy as np

    out = dict(_drawn_inputs(seed))
    spreads = {}
    factors = {'L0_ffn_w_router': 8.0,
     'L0_ffn_corr_bias': 8.0,
     'L0_ffn_gate_w': 8.0,
     'L0_ffn_up_w': 8.0,
     'L0_ffn_down_w': 8.0,
     'L0_ffn_sh_gate_w': 8.0,
     'L0_ffn_sh_up_w': 8.0,
     'L0_ffn_sh_down_w': 8.0}
    for name, (base, spread) in spreads.items():
        noise = np.random.default_rng([zlib.crc32(name.encode()), seed]).standard_normal(out[name].shape)
        drawn = base * np.exp(spread * noise) if base else spread * noise
        out[name] = jnp.asarray(drawn.astype(out[name].dtype))
    for name, factor in factors.items():
        out[name] = (out[name] * factor).astype(out[name].dtype)
    return out
```

```python
import numpy as np
import concourse.bass as bass
from concourse import mybir
from contextlib import ExitStack

P = 128
B, HD, L = 16, 128, 256
NH, DH = 16, 8
BLK = L // P
GB = 4
NG = B // GB
HALF = NH // 2
NP = DH * (DH + 1) // 2
PAIR_AT = [sum(DH - k for k in range(d)) for d in range(DH)]
E, TOPK = 32, 6
NGRP, TOPG = 8, 4
EPG = E // NGRP
M = 176
MH = M // 2
SHM = 2 * M
T = B * HD
KC = L // P
NT = T * TOPK // P + E
LIST = T
ROW = L + 1 + E
TOK_AT, SCORE_AT = L, L + 1
EARLY = 24
EPS = 1e-5

WGU_E = KC * 2 * M
WD_E = 2 * L
WD_AT = E * WGU_E
ARENA = WD_AT + E * WD_E
CTX_AT = EARLY * WGU_E
TOE_AT = CTX_AT + NG * BLK * HD * GB
PROD_AT = TOE_AT + NH * L
PROD_H = BLK * HALF * NP * GB
CONV_AT = PROD_AT + 2 * PROD_H
CONV_H = HALF * BLK * NP * GB
Z_AT = CONV_AT + 2 * CONV_H
Z_SIZE = HALF * BLK * DH * DH * GB
WIDE_AT = Z_AT + Z_SIZE - 3 * P
assert Z_AT + Z_SIZE <= ARENA

WORK = BLK * 4 * GB * P
X2T_AT, SILU_AT, HS_AT = 0, 1024, 1024 + 2 * SHM
HST_AT = HS_AT + 2 * SHM
SHOUT_AT = HST_AT + 4 * P
assert SHOUT_AT + GB * L <= WORK
NX = 4
XT_AT = NX * ROW
SG_AT = XT_AT + 2 * L
H_AT = SG_AT + 2 * M
HT_AT = H_AT + 2 * M
Y_AT = HT_AT + 2 * L
TW_AT = Y_AT + 2 * L
assert TW_AT + 2 <= WORK


def build(nc, x, ctx_t, toeplitz, g_xattn, g_ffn, skip_d, w_router, corr_bias,
          w_gu, w_down, sh_gu, sh_down, out):
    fp32, bf16, u32, i32 = mybir.dt.float32, mybir.dt.bfloat16, mybir.dt.uint32, mybir.dt.int32
    ALU = mybir.AluOpType
    ACT = mybir.ActivationFunctionType
    AX = mybir.AxisListType.X

    lists = nc.dram_tensor("expert_lists", ((E + 1) * LIST, ROW), fp32, kind="Internal").ap()
    sums = [nc.dram_tensor(f"token_sums{i}", (T + P, L), fp32, kind="Internal").ap() for i in range(2)]

    ctx = ExitStack()
    with ctx:
        def sb(name, shape, dt=fp32):
            return ctx.enter_context(nc.sbuf_tensor(name, shape, dt))

        def sem(name):
            return ctx.enter_context(nc.semaphore(name))

        arena = sb("arena", [P, ARENA])
        work = sb("work", [P, WORK])
        rows = sb("rows", [P, B, L])
        shgu_sb = sb("shgu_sb", [P, KC, 2 * SHM])
        shd_sb = sb("shd_sb", [MH, 4, L])
        q_sb = sb("q_sb", [P, NH, BLK, DH, GB])
        payload = sb("payload", [P, GB, ROW])
        blank = sb("blank", [P, ROW])
        ident = sb("ident", [P, P])
        router_sb = sb("router_sb", [P, KC, E])
        bias_sb = sb("bias_sb", [P, E])
        skip_sb = sb("skip_sb", [P, NH])
        gates = sb("gates", [P, 2])
        before_b = sb("before_b", [P, P], bf16)
        ones_b = sb("ones_b", [P, P], bf16)
        mask_b = sb("mask_b", [P, GB, E], bf16)
        seen_b = sb("seen_b", [P, GB + 1, E], bf16)
        lane_dump = sb("lane_dump", [P, 2])
        lane = lane_dump[:, 0:1]
        dump = lane_dump[:, 1:2]
        tok_id = sb("tok_id", [P, B])
        iota_e = sb("iota_e", [P, E])
        list_at = sb("list_at", [P, E])
        tile_at = sb("tile_at", [P, T // P])
        earlier = sb("earlier", [P, NGRP, NGRP])
        slots = sb("slots", [P, GB, DH], u32)
        stats = sb("stats", [P, GB, 6])
        moments = sb("moments", [P, GB, 2])
        newton = sb("newton", [P, 3, GB])
        norm = sb("norm", [P, 2, GB])
        tile_row = sb("tile_row", [P, NT], i32)
        tile_exp = sb("tile_exp", [P, NT], i32)
        tile_dump = sb("tile_dump", [P, NT])
        dest = sb("dest", [P, 2], u32)

        bank = [ctx.enter_context(nc.psum_tensor(f"bank{i}", [P, 512], fp32)) for i in range(8)]

        def win(t, at, dims, parts=P):
            return bass.AP(t, at, [[int(np.prod(t.shape[1:])), parts]] + [list(d) for d in dims])

        ctx_v = win(arena, CTX_AT, [[BLK * HD * GB, NG], [HD * GB, BLK], [DH * GB, NH], [1, DH * GB]])
        toe_v = win(arena, TOE_AT, [[L, NH], [1, L]])
        wgu_v = win(arena, 0, [[1, E * WGU_E]])
        wd_v = win(arena, WD_AT, [[1, E * WD_E]], parts=MH)

        inputs_in = sem("inputs_in")
        consts_done = sem("consts_done")
        iota_done = sem("iota_done")
        toe_done = sem("toe_done")
        tanh_done = sem("tanh_done")
        blank_done = sem("blank_done")
        blanks_stored = sem("blanks_stored")
        vstep = sem("vector_steps")
        ln1_done, xn_ready, qT_ready, q_ready = sem("ln1_done"), sem("xn_ready"), sem("qT_ready"), sem("q_ready")
        products_ready, conv_ready, conv_copied = sem("products_ready"), sem("conv_ready"), sem("conv_copied")
        pairs_summed, attn_ready, ln2_done = sem("pairs_summed"), sem("attn_ready"), sem("ln2_done")
        x2_ready, x2T_ready, x2T_copied = sem("x2_ready"), sem("x2T_ready"), sem("x2T_copied")
        logits_ready, scores_ready = sem("logits_ready"), sem("scores_ready")
        mask_ready, rank_ready, slots_ready = sem("mask_ready"), sem("rank_ready"), sem("slots_ready")
        scattered, payload_free, shared_free = sem("scattered"), sem("payload_free"), sem("shared_free")
        gate_ready, silu_ready, sh_h_ready = sem("gate_ready"), sem("silu_ready"), sem("sh_h_ready")
        sh_hT_ready, sh_hT_copied = sem("sh_hT_ready"), sem("sh_hT_copied")
        sh_ready, sh_copied, sh_stored = sem("sh_ready"), sem("sh_copied"), sem("sh_stored")
        counts_ready, meta_ready, meta_spread, tables_ready = (
            sem("counts_ready"), sem("meta_ready"), sem("meta_spread"), sem("tables_ready"))
        early_in, late_in = sem("early_weights_in"), sem("late_weights_in")
        t_loaded = [sem(f"tile_loaded{i}") for i in range(NX)]
        t_xT, t_xT_copied, t_gu, t_silu, t_h = sem("t_xT"), sem("t_xT_copied"), sem("t_gu"), sem("t_silu"), sem("t_h")
        t_hT, t_hT_copied, t_y, t_y_copied = sem("t_hT"), sem("t_hT_copied"), sem("t_y"), sem("t_y_copied")
        t_wstep = sem("t_weight_steps")
        t_added = [sem(f"tile_added{i}") for i in range(2)]
        sums_in = [sem(f"sums_in{i}") for i in range(NG)]
        f_added, f_done = sem("final_added"), sem("final_done")
        out_stored = sem("out_stored")

        ctx.enter_context(nc.allow_low_precision(reason="small whole numbers, exact in bfloat16"))
        held = sem("held")

        block = ctx.enter_context(nc.Block())

        INPUTS = 16 * 11
        V = 59

        @block.sync
        def _(sp):
            sp.dma_start(rows[:, :, :], x.rearrange("b p l -> p b l")).then_inc(inputs_in, 16)
            sp.dma_start(win(arena, CTX_AT, [[BLK * HD * GB, NG], [1, BLK * HD * GB]]),
                         ctx_t.rearrange("g p n -> p g n")).then_inc(inputs_in, 16)
            sp.dma_start(toe_v, toeplitz).then_inc(inputs_in, 16)
            sp.dma_start(gates[:, 0:1], g_xattn.partition_broadcast(P)).then_inc(inputs_in, 16)
            sp.dma_start(gates[:, 1:2], g_ffn.partition_broadcast(P)).then_inc(inputs_in, 16)
            sp.dma_start(skip_sb[:, :], skip_d.partition_broadcast(P)).then_inc(inputs_in, 16)
            sp.dma_start(bias_sb[:, :], corr_bias.partition_broadcast(P)).then_inc(inputs_in, 16)
            sp.dma_start(router_sb[:, :, :], w_router.rearrange("(c p) e -> p c e", p=P)).then_inc(inputs_in, 16)
            sp.dma_start(shgu_sb[:, :, 0:SHM], sh_gu[0].rearrange("(c p) m -> p c m", p=P)).then_inc(inputs_in, 16)
            sp.dma_start(shgu_sb[:, :, SHM:2 * SHM], sh_gu[1].rearrange("(c p) m -> p c m", p=P)).then_inc(inputs_in, 16)
            sp.dma_start(shd_sb[:, :, :], sh_down.rearrange("(c p) n -> p c n", p=MH)).then_inc(inputs_in, 16)
            sp.wait_ge(blank_done, 1)
            sp.dma_start(bass.AP(lists.tensor, 0, [[ROW, P], [LIST * ROW, E + 1], [1, ROW]]),
                         win(blank, 0, [[0, E + 1], [1, ROW]])).then_inc(blanks_stored, 16)
            sp.dma_start(sums[1].rearrange("(n p) c -> p n c", p=P),
                         win(blank, 0, [[0, T // P + 1], [1, L]])).then_inc(blanks_stored, 16)
            sp.dma_start(sums[0][T:T + P, :], blank[:, 0:L]).then_inc(blanks_stored, 16)
            sp.dma_start(win(arena, 0, [[1, EARLY * WGU_E]]), w_gu[:, 0:EARLY * WGU_E]).then_inc(early_in, 16)
            sp.sem_inc(shared_free, 1)
            with sp.Fori(0, NG) as g:
                sp.wait_ge(sh_copied, g * GB + GB)
                sp.dma_start(sums[0].rearrange("(n p) c -> p n c", p=P)[:, bass.ds(g * GB, GB), :],
                             win(work, SHOUT_AT, [[L, GB], [1, L]])).then_inc(sh_stored, 16)
                sp.wait_ge(sh_stored, g * 16 + 16)
                sp.sem_inc(shared_free, 1)
            sp.wait_ge(pairs_summed, 2 * NG)
            sp.dma_start(win(arena, EARLY * WGU_E, [[1, (E - EARLY) * WGU_E]]),
                         w_gu[:, EARLY * WGU_E:E * WGU_E]).then_inc(late_in, 16)
            sp.wait_ge(tables_ready, 1)
            sp.dma_start(wd_v, w_down).then_inc(late_in, 16)
            sp.wait_ge(t_added[0], 16 * (NT // 2))
            sp.wait_ge(t_added[1], 16 * (NT // 2))
            for c in range(NG):
                for i in range(2):
                    sp.dma_start(win(arena, (2 * c + i) * GB * L, [[L, GB], [1, L]]),
                                 sums[i].rearrange("(n p) c -> p n c", p=P)[:, c * GB:(c + 1) * GB, :]
                                 ).then_inc(sums_in[c], 16)
            for c in range(NG):
                sp.wait_ge(f_done, c + 1)
                sp.dma_start(out.rearrange("b p l -> p b l")[:, c * GB:(c + 1) * GB, :],
                             win(arena, 2 * c * GB * L, [[L, GB], [1, L]])).then_inc(out_stored, 16)
            sp.wait_ge(out_stored, 16 * NG)

        @block.gpsimd
        def _(pool):
            step = [0]

            def link(ins):
                step[0] += 1
                ins.then_inc(iota_done, 1)
                pool.wait_ge(iota_done, step[0])

            iota_i = win(work, 0, [[1, 1 + E]]).bitcast(i32)
            nc.gpsimd.memset(ident[:, :], 0.0)
            nc.gpsimd.memset(before_b[:, :], 0.0)
            nc.gpsimd.memset(ones_b[:, :], 1.0)
            nc.gpsimd.memset(seen_b[:, :, :], 0.0)
            link(nc.gpsimd.memset(earlier[:, :, :], 0.0))
            nc.gpsimd.affine_select(out=ident[:, :], in_=ident[:, :], compare_op=ALU.not_equal, fill=1.0,
                                    base=0, pattern=[[-1, P]], channel_multiplier=1)
            nc.gpsimd.affine_select(out=before_b[:, :], in_=before_b[:, :], compare_op=ALU.is_ge, fill=1.0,
                                    base=0, pattern=[[-1, P]], channel_multiplier=1)
            nc.gpsimd.affine_select(out=earlier[:, :, :], in_=earlier[:, :, :], compare_op=ALU.is_ge, fill=1.0,
                                    base=0, pattern=[[-1, NGRP], [1, NGRP]], channel_multiplier=0)
            nc.gpsimd.iota(iota_i[:, 0:1], pattern=[[0, 1]], base=0, channel_multiplier=1)
            link(nc.gpsimd.iota(iota_i[:, 1:33], pattern=[[1, E]], base=0, channel_multiplier=0))
            nc.gpsimd.tensor_copy(lane[:, :], iota_i[:, 0:1])
            link(nc.gpsimd.tensor_copy(iota_e[:, :], iota_i[:, 1:33]))
            nc.gpsimd.tensor_scalar(dump[:, :], lane[:, :], float(T), None, ALU.add)
            nc.gpsimd.tensor_scalar(list_at[:, :], iota_e[:, :], float(LIST), None, ALU.mult)
            link(nc.gpsimd.tensor_scalar(tile_at[:, :], iota_e[:, 0:T // P], float(P), None, ALU.mult))
            link(nc.gpsimd.tensor_scalar(tok_id[:, :], tile_at[:, :], lane[:, 0:1], None, ALU.add))
            nc.gpsimd.memset(blank[:, :], 0.0).then_inc(consts_done, 1)
            pool.wait_ge(consts_done, 1)
            nc.gpsimd.tensor_copy(blank[:, TOK_AT:TOK_AT + 1], dump[:, :]).then_inc(blank_done, 1)

            pool.wait_ge(blanks_stored, 48)
            pool.sem_inc(payload_free, 1)
            with pool.Fori(0, NG) as g:
                pool.wait_ge(slots_ready, g + 1)
                pool.sem_inc(held, 1)
                for b in range(GB):
                    for k in range(TOPK):
                        nc.gpsimd.indirect_dma_start(
                            lists, bass.IndirectOffsetOnAxis(ap=slots[:, b, k:k + 1], axis=0),
                            payload[:, b, :], None).then_inc(scattered, 16)
                pool.wait_ge(scattered, (g + 1) * (GB * TOPK * 16))
                pool.sem_inc(payload_free, 1)

            def add_tile(t, u):
                pool.wait_ge(t_y_copied, t + 1)
                pool.wait_ge(t_wstep, t + 1)
                if not (isinstance(t, int) and t < 2):
                    pool.wait_ge(t_added[u % 2], t // 2 * 16 if isinstance(t, int) else (t - u % 2) * 8)
                pool.sem_inc(held, 1)
                nc.gpsimd.indirect_dma_start(
                    sums[u % 2], bass.IndirectOffsetOnAxis(ap=dest[:, u % 2:u % 2 + 1], axis=0),
                    win(work, Y_AT + (u % 2) * L, [[1, L]]), None,
                    compute_op=ALU.add).then_inc(t_added[u % 2], 16)

            pool.wait_ge(sh_stored, 16 * NG)
            for t in range(4):
                add_tile(t, t % 4)
            with pool.Fori(1, NT // 4) as n:
                for u in range(4):
                    add_tile(n * 4 + u, u)

        @block.scalar
        def _(act):
            act.wait_ge(inputs_in, INPUTS)
            nc.scalar.activation(gates[:, :], gates[:, :], ACT.Tanh).then_inc(tanh_done, 1)
            with act.Fori(0, NG) as g:
                act.wait_ge(ln1_done, g + 1)
                act.sem_inc(held, 1)
                for b in range(GB):
                    last = nc.scalar.activation(win(work, b * L, [[1, L]]), rows[:, bass.ds(g * GB + b, 1), :],
                                                ACT.Identity, bias=norm[:, 1, b:b + 1], scale=norm[:, 0, b:b + 1])
                last.then_inc(xn_ready, 1)
                for p in range(2):
                    act.wait_ge(qT_ready, g * 2 + p + 1)
                    for b in range(2):
                        last = nc.scalar.copy(
                            win(q_sb, 2 * p + b, [[DH * GB, BLK], [BLK * DH * GB, NH], [GB, DH]]),
                            win(bank[p], b * L, [[P, BLK], [DH, NH], [1, DH]]))
                last.then_inc(q_ready, 1)
                for h in range(NH):
                    act.wait_ge(conv_ready, g * NH + h + 1)
                    nc.scalar.copy(win(arena, CONV_AT + h * BLK * NP * GB, [[1, BLK * NP * GB]]),
                                   bank[2 + h % 2][:, 0:BLK * NP * GB]).then_inc(conv_copied, 1)
                act.wait_ge(ln2_done, g + 1)
                act.wait_ge(payload_free, g + 1)
                act.sem_inc(held, 1)
                for b in range(GB):
                    last = nc.scalar.activation(payload[:, b, 0:L], rows[:, bass.ds(g * GB + b, 1), :],
                                                ACT.Identity, bias=norm[:, 1, b:b + 1], scale=norm[:, 0, b:b + 1])
                last.then_inc(x2_ready, 1)
                for p in range(2):
                    act.wait_ge(x2T_ready, g * 2 + p + 1)
                    nc.scalar.copy(win(work, X2T_AT + p * 512, [[1, 512]]), bank[p][:, :]).then_inc(x2T_copied, 1)
                act.wait_ge(logits_ready, g + 1)
                nc.scalar.activation(payload[:, :, SCORE_AT:ROW], win(bank[4], 0, [[E, GB], [1, E]]),
                                     ACT.Sigmoid).then_inc(scores_ready, 1)

                def shared_silu(b):
                    act.wait_ge(gate_ready, g * GB + b + 1)
                    nc.scalar.activation(win(work, SILU_AT + b % 2 * SHM, [[1, SHM]]), bank[5][:, 0:SHM],
                                         ACT.Silu).then_inc(silu_ready, 1)

                for b in range(GB):
                    shared_silu(b)
                    act.wait_ge(sh_hT_ready, g * GB + b + 1)
                    nc.scalar.copy(win(work, HST_AT, [[1, 512]], parts=MH), bank[7][0:MH, :]).then_inc(sh_hT_copied, 1)
                    act.wait_ge(sh_ready, g * GB + b + 1)
                    nc.scalar.copy(win(work, SHOUT_AT + b * L, [[1, L]]), bank[2 + b % 2][:, 0:L]).then_inc(sh_copied, 1)

            act.wait_ge(tables_ready, 1)
            act.wait_ge(payload_free, NG + 1)
            act.wait_ge(sh_stored, 16 * NG)

            def load_tile(t, u):
                first = act.value_load(tile_row[0:1, bass.ds(t, 1)], min_val=0, max_val=E * LIST)
                if not (isinstance(t, int) and t < NX):
                    act.wait_ge(t_wstep, t - NX + 1)
                    act.wait_ge(t_xT, t - NX + 1)
                act.dma_start(win(work, u * ROW, [[1, ROW]]), lists[bass.ds(first, P), :]).then_inc(t_loaded[u], 16)

            def copy_xT(t, u):
                act.wait_ge(t_xT, t + 1)
                nc.scalar.copy(win(work, XT_AT + u % 2 * L, [[1, L]]), bank[u % 2][:, 0:L]).then_inc(t_xT_copied, 1)

            def silu(t, u):
                act.wait_ge(t_gu, t + 1)
                nc.scalar.activation(win(work, SG_AT + u % 2 * M, [[1, M]]), bank[2 + u % 2][:, 0:M],
                                     ACT.Silu).then_inc(t_silu, 1)

            def copy_y(t, u):
                act.wait_ge(t_y, t + 1)
                if not (isinstance(t, int) and t < 2):
                    act.wait_ge(t_added[u % 2], t // 2 * 16 if isinstance(t, int) else (t - u % 2) * 8)
                nc.scalar.copy(win(work, Y_AT + u % 2 * L, [[1, L]]), bank[6 + u % 2][:, 0:L]).then_inc(t_y_copied, 1)

            def tile_step(t, u, lo=0, hi=NT):
                if not isinstance(t, int) or t + 1 < NT:
                    copy_xT(t + 1, (u + 1) % 4)
                if not isinstance(t, int) or t + 3 < NT and t >= 1:
                    load_tile(t + 3, (u + 3) % 4)
                if not isinstance(t, int) or t < NT:
                    silu(t, u)
                if not isinstance(t, int) or t >= 2:
                    copy_y(t - 2, (u + 2) % 4)

            for t in range(4):
                load_tile(t, t)
            copy_xT(0, 0)
            for t in range(4):
                tile_step(t, t)
            with act.Fori(1, NT // 4 - 1) as n:
                for u in range(4):
                    tile_step(n * 4 + u, u)
            for t in range(NT - 4, NT + 2):
                tile_step(t, t % 4)

        @block.vector
        def _(dve):
            count = [0]

            dve.wait_ge(inputs_in, INPUTS)
            dve.wait_ge(iota_done, 5)
            nc.vector.tensor_tensor(win(arena, Z_AT, [[P, NH], [1, P]]), win(ident, 0, [[0, NH], [1, P]]),
                                    win(skip_sb, 0, [[1, NH], [0, P]]), ALU.mult).then_inc(toe_done, 1)
            dve.wait_ge(toe_done, 1)
            toe_diag = win(arena, TOE_AT, [[L, NH], [1, P]])
            nc.vector.tensor_tensor(toe_diag, toe_diag, win(arena, Z_AT, [[P, NH], [1, P]]), ALU.add).then_inc(toe_done, 1)
            dve.wait_ge(tanh_done, 1)

            with dve.Fori(0, NG) as g:
                count[0] = 0

                def link(ins, hold=False):
                    count[0] += 1
                    ins.then_inc(vstep, 1)
                    dve.wait_ge(vstep, g * V + count[0])
                    if hold:
                        dve.sem_inc(held, 1)

                def layernorm(done):
                    for b in range(GB):
                        last = nc.vector.bn_stats(stats[:, b, :], rows[:, bass.ds(g * GB + b, 1), :].rearrange("p a l -> p (a l)"))
                    link(last, hold=True)
                    for b in range(GB):
                        last = nc.vector.bn_aggr(moments[:, b, :], stats[:, b, :])
                    link(last)
                    v, y, z = newton[:, 0, :], newton[:, 1, :], newton[:, 2, :]
                    link(nc.vector.tensor_scalar(v, moments[:, :, 1], EPS, None, ALU.add))
                    link(nc.vector.tensor_scalar(y.bitcast(i32), v.bitcast(i32), -0.5, float(0x5F3759DF),
                                                 ALU.mult, ALU.add))
                    for n in range(4):
                        link(nc.vector.tensor_tensor(z, y, y, ALU.mult))
                        link(nc.vector.scalar_tensor_tensor(z, z, -0.5, v, ALU.mult, ALU.mult))
                        r = norm[:, 0, :] if n == 3 else y
                        link(nc.vector.scalar_tensor_tensor(r, z, 1.5, y, ALU.add, ALU.mult))
                    nc.vector.scalar_tensor_tensor(norm[:, 1, :], moments[:, :, 0], -1.0, norm[:, 0, :],
                                                   ALU.mult, ALU.mult).then_inc(done, 1)

                layernorm(ln1_done)
                for s in range(2):
                    for d in range(DH):
                        n = (DH - d) * GB
                        c = ctx_v[:, bass.ds(g, 1), :, s * HALF:(s + 1) * HALF, :].rearrange("p a k h n -> p (a k) h n")
                        last = nc.vector.tensor_tensor(
                            win(arena, PROD_AT + s * PROD_H + PAIR_AT[d] * GB,
                                [[HALF * NP * GB, BLK], [NP * GB, HALF], [1, n]]),
                            c[:, :, :, 0:n], c[:, :, :, d * GB:d * GB + n], ALU.mult)
                    last.then_inc(products_ready, 1)
                dve.wait_ge(q_ready, g + 1)
                HB = HALF * BLK
                for s in range(2):
                    dve.wait_ge(conv_copied, g * NH + (s + 1) * HALF)
                    for d in range(DH):
                        y = win(arena, CONV_AT + s * CONV_H + PAIR_AT[d] * GB, [[NP * GB, HB], [GB, DH - d], [1, GB]])
                        for i0, z0 in ((0, d * GB), (d, d * DH * GB)) if d else ((0, 0),):
                            last = nc.vector.tensor_tensor(
                                win(arena, Z_AT + z0, [[DH * DH * GB, HB], [(DH + 1) * GB, DH - d], [1, GB]]),
                                y, win(q_sb, s * HB * DH * GB + i0 * GB, [[DH * GB, HB], [GB, DH - d], [1, GB]]),
                                ALU.mult)
                    link(last)
                    if s == 0:
                        dve.wait_ge(shared_free, g + 1)
                    ZH = DH * DH * GB
                    for k in range(BLK):
                        for i in range(4):
                            z = [win(arena, Z_AT + k * ZH + ii * DH * GB, [[BLK * ZH, HALF], [GB, DH], [1, GB]])
                                 for ii in (i, i + 4)]
                            last = nc.vector.tensor_tensor(
                                win(work, (k * 4 + i) * GB * P + s * HALF * DH, [[DH, HALF], [1, DH], [P, GB]]),
                                z[0], z[1], ALU.add)
                    last.then_inc(pairs_summed, 1)
                    dve.wait_ge(pairs_summed, g * 2 + s + 1)
                for p in range(2):
                    dve.wait_ge(attn_ready, g * 2 + p + 1)
                    r = rows[:, bass.ds(g * GB + 2 * p, 2), :].rearrange("p b l -> p (b l)")
                    last = nc.vector.scalar_tensor_tensor(r, bank[p][:, :], gates[:, 0:1], r, ALU.mult, ALU.add)
                link(last, hold=True)
                layernorm(ln2_done)

                dve.wait_ge(scores_ready, g + 1)
                nc.vector.tensor_copy(payload[:, :, TOK_AT], tok_id[:, bass.ds(g * GB, GB)])
                at = [Z_AT]

                def tmp(*shape):
                    n = int(np.prod(shape))
                    o = at[0]
                    at[0] += n
                    return o

                def flat(o, n, step=1):
                    return win(arena, o, [[step, n]])

                scores = payload[:, :, SCORE_AT:ROW]
                sfc = tmp(GB, E)
                link(nc.vector.tensor_tensor(win(arena, sfc, [[E, GB], [1, E]]), scores,
                                             win(bias_sb, 0, [[0, GB], [1, E]]), ALU.add))
                NP2 = GB * E // 2
                hi2, lo2 = tmp(NP2), tmp(NP2)
                nc.vector.tensor_tensor(flat(hi2, NP2), flat(sfc, NP2, 2), flat(sfc + 1, NP2, 2), ALU.max)
                link(nc.vector.tensor_tensor(flat(lo2, NP2), flat(sfc, NP2, 2), flat(sfc + 1, NP2, 2), ALU.min))
                G4 = GB * NGRP
                best, a2, c2, gs = tmp(G4), tmp(G4), tmp(G4), tmp(G4)
                nc.vector.tensor_tensor(flat(best, G4), flat(hi2, G4, 2), flat(hi2 + 1, G4, 2), ALU.max)
                nc.vector.tensor_tensor(flat(a2, G4), flat(hi2, G4, 2), flat(hi2 + 1, G4, 2), ALU.min)
                link(nc.vector.tensor_tensor(flat(c2, G4), flat(lo2, G4, 2), flat(lo2 + 1, G4, 2), ALU.max))
                link(nc.vector.tensor_tensor(flat(a2, G4), flat(a2, G4), flat(c2, G4), ALU.max))
                link(nc.vector.tensor_tensor(flat(gs, G4), flat(best, G4), flat(a2, G4), ALU.add))
                cmp, eq = tmp(GB, NGRP, NGRP), tmp(GB, NGRP, NGRP)
                dims = [[NGRP * NGRP, GB], [NGRP, NGRP], [1, NGRP]]
                other = win(arena, gs, [[NGRP, GB], [0, NGRP], [1, NGRP]])
                own = win(arena, gs, [[NGRP, GB], [1, NGRP], [0, NGRP]])
                nc.vector.tensor_tensor(win(arena, cmp, dims), other, own, ALU.is_gt)
                link(nc.vector.tensor_tensor(win(arena, eq, dims), other, own, ALU.is_equal))
                link(nc.vector.tensor_tensor(win(arena, eq, dims), win(arena, eq, dims),
                                             win(earlier, 0, [[0, GB], [NGRP, NGRP], [1, NGRP]]), ALU.mult))
                link(nc.vector.tensor_tensor(flat(cmp, GB * 64), flat(cmp, GB * 64), flat(eq, GB * 64), ALU.add))
                grank, keep, off = tmp(G4), tmp(G4), tmp(G4)
                link(nc.vector.tensor_reduce(flat(grank, G4), win(arena, cmp, [[NGRP, G4], [1, NGRP]]), AX, ALU.add))
                link(nc.vector.tensor_scalar(flat(keep, G4), flat(grank, G4), float(TOPG), None, ALU.is_lt))
                link(nc.vector.tensor_scalar(flat(off, G4), flat(keep, G4), -1.0, 1e30, ALU.add, ALU.mult))
                each = lambda o: win(arena, o, [[1, G4], [0, EPG]])
                four = lambda o: win(arena, o, [[EPG, G4], [1, EPG]])
                masked = tmp(GB, E)
                link(nc.vector.tensor_tensor(four(masked), four(sfc), each(keep), ALU.mult))
                link(nc.vector.tensor_tensor(four(masked), four(masked), each(off), ALU.add), hold=True)
                top, top_i, top_f = tmp(GB, 8), tmp(GB, 8), tmp(GB, 8)
                idx = lambda o, n: win(arena, o, [[1, n]]).bitcast(u32)
                for b in range(GB):
                    last = nc.vector.max(flat(top + 8 * b, 8), flat(masked + E * b, E))
                link(last, hold=True)
                for b in range(GB):
                    last = nc.vector.max_index(idx(top_i + 8 * b, 8), flat(top + 8 * b, 8), flat(masked + E * b, E))
                link(last)
                link(nc.vector.tensor_copy(flat(top_f, 8 * GB), idx(top_i, 8 * GB)))
                onehot, part = tmp(GB, TOPK, E), tmp(GB, TOPK, E)
                bke = [[TOPK * E, GB], [E, TOPK], [1, E]]
                link(nc.vector.tensor_tensor(win(arena, onehot, bke), win(iota_e, 0, [[0, GB], [0, TOPK], [1, E]]),
                                             win(arena, top_f, [[8, GB], [1, TOPK], [0, E]]), ALU.is_equal))
                link(nc.vector.tensor_reduce(mask_b[:, :, :], win(arena, onehot, [[TOPK * E, GB], [1, E], [E, TOPK]]),
                                             AX, ALU.add))
                for b in range(GB):
                    ins = nc.vector.tensor_tensor(seen_b[:, b + 1, :], seen_b[:, b, :], mask_b[:, b, :], ALU.add)
                    link(ins) if b + 1 < GB else ins.then_inc(mask_ready, 1)
                dve.wait_ge(mask_ready, g + 1)
                dve.wait_ge(rank_ready, g + 1)
                nc.vector.tensor_copy(seen_b[:, 0, :], seen_b[:, GB, :])
                place = tmp(GB, E)
                link(nc.vector.tensor_tensor(win(arena, place, [[E, GB], [1, E]]), win(bank[4], GB * E, [[E, GB], [1, E]]),
                                             win(list_at, 0, [[0, GB], [1, E]]), ALU.add))
                link(nc.vector.tensor_tensor(win(arena, part, bke), win(arena, onehot, bke),
                                             win(arena, place, [[E, GB], [0, TOPK], [1, E]]), ALU.mult))
                slot_f = tmp(GB, TOPK)
                link(nc.vector.tensor_reduce(win(arena, slot_f, [[1, GB * TOPK]]), win(arena, part, [[E, GB * TOPK], [1, E]]),
                                             AX, ALU.add))
                nc.vector.tensor_copy(slots[:, :, 0:TOPK], win(arena, slot_f, [[TOPK, GB], [1, TOPK]])).then_inc(slots_ready, 1)
                for b in range(GB):
                    dve.wait_ge(silu_ready, g * GB + b + 1)
                    nc.vector.tensor_tensor(win(work, HS_AT + b % 2 * SHM, [[1, SHM]]),
                                            win(work, SILU_AT + b % 2 * SHM, [[1, SHM]]), bank[6][:, 0:SHM],
                                            ALU.mult).then_inc(sh_h_ready, 1)
                assert count[0] == V, count[0]

            base = [NG * V]

            def chain(ins):
                base[0] += 1
                ins.then_inc(vstep, 1)
                dve.wait_ge(vstep, base[0])

            at = [Z_AT]

            def tmp(n):
                at[0] += n
                return at[0] - n

            def flat(o, n=1):
                return win(arena, o, [[1, n]])

            cnt, cmp, nt = tmp(E), tmp(E * (T // P)), tmp(E)
            PAD = E // 2
            run = [tmp(PAD + E), tmp(PAD + E)]
            nc.vector.memset(flat(run[0], PAD), 0.0)
            nc.vector.memset(flat(run[1], PAD), 0.0)
            dve.wait_ge(counts_ready, 1)
            chain(nc.vector.tensor_copy(flat(cnt, E), bank[4][:, 0:E]))
            chain(nc.vector.tensor_tensor(win(arena, cmp, [[T // P, E], [1, T // P]]), win(arena, cnt, [[1, E], [0, T // P]]),
                                          win(tile_at, 0, [[0, E], [1, T // P]]), ALU.is_gt))
            chain(nc.vector.tensor_reduce(flat(nt, E), win(arena, cmp, [[T // P, E], [1, T // P]]), AX, ALU.add))
            chain(nc.vector.tensor_copy(flat(run[0] + PAD, E), flat(nt, E)))
            s, src = 1, 0
            while s < E:
                chain(nc.vector.tensor_tensor(flat(run[1 - src] + PAD, E), flat(run[src] + PAD, E),
                                              flat(run[src] + PAD - s, E), ALU.add))
                s, src = 2 * s, 1 - src
            past, pn, ex, first, n_e, c1 = tmp(E), tmp(E), tmp(1), tmp(1), tmp(1), tmp(1)
            chain(nc.vector.tensor_scalar(flat(past, E), flat(run[src] + PAD, E), lane[:, 0:1], None, ALU.is_le))
            chain(nc.vector.tensor_tensor(flat(pn, E), flat(past, E), flat(nt, E), ALU.mult))
            nc.vector.tensor_reduce(flat(ex), flat(past, E), AX, ALU.add)
            chain(nc.vector.tensor_reduce(flat(first), flat(pn, E), AX, ALU.add))
            chain(nc.vector.tensor_scalar(flat(past, E), iota_e[:, :], flat(ex), None, ALU.is_equal))
            chain(nc.vector.tensor_tensor(flat(pn, E), flat(past, E), flat(cnt, E), ALU.mult))
            chain(nc.vector.tensor_reduce(flat(n_e), flat(pn, E), AX, ALU.add))
            off, top, start, meta = tmp(1), tmp(1), tmp(1), tmp(3)
            chain(nc.vector.tensor_scalar(flat(off), lane[:, :], flat(first), float(P), ALU.subtract, ALU.mult))
            chain(nc.vector.tensor_scalar(flat(top), flat(n_e), -float(P), 0.0, ALU.add, ALU.max))
            chain(nc.vector.tensor_tensor(flat(start), flat(off), flat(top), ALU.min))
            chain(nc.vector.scalar_tensor_tensor(flat(meta), flat(ex), float(LIST), flat(start), ALU.mult, ALU.add))
            chain(nc.vector.tensor_scalar(flat(meta + 1), flat(ex), float(E - 1), None, ALU.min))
            chain(nc.vector.tensor_tensor(flat(meta + 2), flat(off), flat(start), ALU.subtract))
            assert at[0] <= WIDE_AT
            nc.vector.tensor_copy(win(arena, WIDE_AT, [[P, 3], [1, P]]), win(arena, meta, [[1, 3], [0, P]])).then_inc(meta_ready, 1)
            dve.wait_ge(meta_spread, 1)
            nc.vector.tensor_copy(tile_row[:, :], bank[5][:, 0:P])
            nc.vector.tensor_copy(tile_exp[:, :], bank[5][:, P:2 * P])
            nc.vector.tensor_scalar(tile_dump[:, :], bank[5][:, 2 * P:3 * P], lane[:, 0:1], dump[:, 0:1],
                                    ALU.is_gt, ALU.mult).then_inc(tables_ready, 1)

            dve.wait_ge(tables_ready, 1)

            def times(t, u):
                e = dve.value_load(tile_exp[0:1, bass.ds(t, 1)], min_val=0, max_val=E - 1)
                dve.wait_ge(t_loaded[u], (t // 4 + 1) * 16 if isinstance(t, int) else (t - u) * 4 + 16)
                x_at = u * ROW
                w = win(work, TW_AT + u % 2, [[1, 1]])
                nc.vector.tensor_copy(w, win(work, x_at + SCORE_AT, [[1, E]])[:, bass.ds(e, 1)])
                if not (isinstance(t, int) and t < 2):
                    dve.wait_ge(t_added[u % 2], t // 2 * 16 if isinstance(t, int) else (t - u % 2) * 8)
                nc.vector.tensor_tensor(dest[:, u % 2:u % 2 + 1], win(work, x_at + TOK_AT, [[1, 1]]),
                                        tile_dump[:, bass.ds(t, 1)], ALU.max).then_inc(t_wstep, 1)
                dve.wait_ge(t_wstep, t + 1)
                dve.wait_ge(t_silu, t + 1)
                nc.vector.scalar_tensor_tensor(win(work, H_AT + u % 2 * M, [[1, M]]), win(work, SG_AT + u % 2 * M, [[1, M]]),
                                               w, bank[2 + u % 2][:, M:2 * M], ALU.mult, ALU.mult).then_inc(t_h, 1)

            def copy_hT(t, u):
                dve.wait_ge(t_hT, t + 1)
                nc.vector.tensor_copy(win(work, HT_AT + u % 2 * L, [[1, L]], parts=MH),
                                      bank[4 + u % 2][0:MH, 0:L]).then_inc(t_hT_copied, 1)

            def tile_step(t, u):
                if not isinstance(t, int) or t < NT:
                    times(t, u)
                if not isinstance(t, int) or 1 <= t <= NT:
                    copy_hT(t - 1, (u + 3) % 4)

            for t in range(4):
                tile_step(t, t)
            with dve.Fori(1, NT // 4 - 1) as n:
                for u in range(4):
                    tile_step(n * 4 + u, u)
            for t in range(NT - 4, NT + 1):
                tile_step(t, t % 4)

            for c in range(NG):
                a = win(arena, 2 * c * GB * L, [[1, GB * L]])
                b = win(arena, (2 * c + 1) * GB * L, [[1, GB * L]])
                dve.wait_ge(sums_in[c], 32)
                nc.vector.tensor_tensor(a, a, b, ALU.add).then_inc(f_added, 1)
                dve.wait_ge(f_added, c + 1)
                nc.vector.scalar_tensor_tensor(a, a, gates[:, 1:2],
                                               rows[:, c * GB:(c + 1) * GB, :].rearrange("p b l -> p (b l)"),
                                               ALU.mult, ALU.add).then_inc(f_done, 1)

        @block.tensor
        def _(pe):
            pe.wait_ge(inputs_in, INPUTS)
            pe.wait_ge(iota_done, 5)
            pe.wait_ge(toe_done, 2)
            prods = lambda s, h, k, n: win(arena, PROD_AT + s * PROD_H + (k * HALF + h) * NP * GB,
                                           [[HALF * NP * GB, n], [1, NP * GB]])
            toe = lambda h, a: win(arena, TOE_AT + h * L + a * P, [[1, P]])
            CB = NP * GB
            with pe.Fori(0, NG) as g:
                pe.wait_ge(xn_ready, g + 1)
                for p in range(2):
                    for b in range(2):
                        for k in range(BLK):
                            last = nc.tensor.transpose(bank[p][:, (b * BLK + k) * P:(b * BLK + k + 1) * P],
                                                       win(work, (2 * p + b) * L + k * P, [[1, P]]), ident[:, :])
                    last.then_inc(qT_ready, 1)
                for h in range(NH):
                    s, hh = divmod(h, HALF)
                    if hh == 0:
                        pe.wait_ge(products_ready, g * 2 + s + 1)
                    if h >= 2:
                        pe.wait_ge(conv_copied, g * NH + h - 1)
                    y = bank[2 + h % 2]
                    nc.tensor.matmul(y[:, 0:2 * CB], toe(h, 0), prods(s, hh, 0, 2), start=True, stop=False)
                    nc.tensor.matmul(y[:, CB:2 * CB], toe(h, 1), prods(s, hh, 0, 1), start=False,
                                     stop=True).then_inc(conv_ready, 1)
                pe.wait_ge(pairs_summed, g * 2 + 2)
                for p in range(2):
                    for b in range(2):
                        for k in range(BLK):
                            for i in range(4):
                                last = nc.tensor.matmul(
                                    bank[p][:, (b * BLK + k) * P:(b * BLK + k + 1) * P],
                                    win(work, ((k * 4 + i) * GB + 2 * p + b) * P, [[1, P]]), ident[:, :],
                                    start=(i == 0), stop=(i == 3))
                    last.then_inc(attn_ready, 1)
                pe.wait_ge(x2_ready, g + 1)
                for p in range(2):
                    for b in range(2):
                        for k in range(KC):
                            last = nc.tensor.transpose(bank[p][:, (b * KC + k) * P:(b * KC + k + 1) * P],
                                                       payload[:, 2 * p + b, k * P:(k + 1) * P], ident[:, :])
                    last.then_inc(x2T_ready, 1)
                x2T = lambda b, k: win(work, X2T_AT + (b * KC + k) * P, [[1, P]])
                pe.wait_ge(x2T_copied, g * 2 + 2)
                for b in range(GB):
                    for k in range(KC):
                        last = nc.tensor.matmul(bank[4][:, b * E:(b + 1) * E], x2T(b, k), router_sb[:, k, :],
                                                start=(k == 0), stop=(k == KC - 1))
                last.then_inc(logits_ready, 1)

                def shared_up(b):
                    if b:
                        pe.wait_ge(sh_h_ready, g * GB + b)
                    for half in range(2):
                        for k in range(KC):
                            last = nc.tensor.matmul(bank[5 + half][:, 0:SHM], x2T(b, k),
                                                    shgu_sb[:, k, half * SHM:(half + 1) * SHM],
                                                    start=(k == 0), stop=(k == KC - 1))
                    last.then_inc(gate_ready, 1)

                for b in range(GB):
                    shared_up(b)
                    if b == 0:
                        pe.wait_ge(mask_ready, g + 1)
                        nc.tensor.matmul(bank[4][:, GB * E:2 * GB * E], before_b[:, :],
                                         mask_b[:, :, :].rearrange("p b e -> p (b e)"), start=True, stop=False)
                        nc.tensor.matmul(bank[4][:, GB * E:2 * GB * E], ones_b[:, :],
                                         seen_b[:, 0:GB, :].rearrange("p b e -> p (b e)"), start=False,
                                         stop=True).then_inc(rank_ready, 1)
                    pe.wait_ge(sh_h_ready, g * GB + b + 1)
                    for c in range(4):
                        last = nc.tensor.transpose(bank[7][0:MH, c * P:(c + 1) * P],
                                                   win(work, HS_AT + b % 2 * SHM + c * MH, [[1, MH]]), ident[:, :])
                    last.then_inc(sh_hT_ready, 1)
                    pe.wait_ge(sh_hT_copied, g * GB + b + 1)
                    for c in range(4):
                        last = nc.tensor.matmul(bank[2 + b % 2][:, 0:L], win(work, HST_AT + c * P, [[1, P]], parts=MH),
                                                shd_sb[:, c, :], start=(c == 0), stop=(c == 3))
                    last.then_inc(sh_ready, 1)

            pe.wait_ge(slots_ready, NG)
            nc.tensor.matmul(bank[4][:, 0:E], ones_b[:, :], seen_b[:, 0, :], start=True, stop=True).then_inc(counts_ready, 1)
            pe.wait_ge(meta_ready, 1)
            for c in range(3):
                last = nc.tensor.matmul(bank[5][:, c * P:(c + 1) * P], win(arena, WIDE_AT + c * P, [[1, P]]), ident[:, :],
                                        start=True, stop=True)
            last.then_inc(meta_spread, 1)

            pe.wait_ge(tables_ready, 1)
            pe.wait_ge(early_in, 16)
            pe.wait_ge(late_in, 32)

            def xT(t, u):
                pe.wait_ge(t_loaded[u], (t // 4 + 1) * 16 if isinstance(t, int) else (t - u) * 4 + 16)
                if not (isinstance(t, int) and t < 2):
                    pe.wait_ge(t_xT_copied, t - 1)
                for k in range(KC):
                    last = nc.tensor.transpose(bank[u % 2][:, k * P:(k + 1) * P],
                                               win(work, u * ROW + k * P, [[1, P]]), ident[:, :])
                last.then_inc(t_xT, 1)

            def gate_up(t, u, e):
                pe.wait_ge(t_xT_copied, t + 1)
                if not (isinstance(t, int) and t < 2):
                    pe.wait_ge(t_h, t - 1)
                for k in range(KC):
                    last = nc.tensor.matmul(bank[2 + u % 2][:, 0:2 * M], win(work, XT_AT + u % 2 * L + k * P, [[1, P]]),
                                            wgu_v[:, bass.ds(e * WGU_E + k * 2 * M, 2 * M)],
                                            start=(k == 0), stop=(k == KC - 1))
                last.then_inc(t_gu, 1)

            def hT(t, u):
                pe.wait_ge(t_h, t + 1)
                if not (isinstance(t, int) and t < 2):
                    pe.wait_ge(t_hT_copied, t - 1)
                for c in range(2):
                    last = nc.tensor.transpose(bank[4 + u % 2][0:MH, c * P:(c + 1) * P],
                                               win(work, H_AT + u % 2 * M + c * MH, [[1, MH]]), ident[:, :])
                last.then_inc(t_hT, 1)

            def down(t, u, e):
                pe.wait_ge(t_hT_copied, t + 1)
                if not (isinstance(t, int) and t < 2):
                    pe.wait_ge(t_y_copied, t - 1)
                for c in range(2):
                    last = nc.tensor.matmul(bank[6 + u % 2][:, 0:L], win(work, HT_AT + u % 2 * L + c * P, [[1, P]], parts=MH),
                                            wd_v[:, bass.ds(e * WD_E + c * L, L)],
                                            start=(c == 0), stop=(c == 1))
                last.then_inc(t_y, 1)

            def expert(t):
                return pe.value_load(tile_exp[0:1, bass.ds(t, 1)], min_val=0, max_val=E - 1)

            def tile_step(t, u):
                if not isinstance(t, int) or t + 1 < NT:
                    xT(t + 1, (u + 1) % 4)
                if not isinstance(t, int) or t < NT:
                    gate_up(t, u, expert(t))
                if not isinstance(t, int) or 1 <= t <= NT:
                    hT(t - 1, (u + 3) % 4)
                if not isinstance(t, int) or t >= 2:
                    down(t - 2, (u + 2) % 4, expert(t - 2))

            xT(0, 0)
            for t in range(4):
                tile_step(t, t)
            with pe.Fori(1, NT // 4 - 1) as n:
                for u in range(4):
                    tile_step(n * 4 + u, u)
            for t in range(NT - 4, NT + 2):
                tile_step(t, t % 4)


def toeplitz_layout(kern):
    kern = np.asarray(kern)
    padded = np.concatenate([np.zeros((NH, P), kern.dtype), kern], axis=1)
    at = P + np.arange(L)[None, :] - np.arange(P)[:, None]
    return np.ascontiguousarray(padded[:, at].transpose(1, 0, 2)).reshape(P, NH * L)


def kernel(x, ctx_2048, g_xattn, g_ffn, L0_xattn_ssm_kernel, L0_xattn_D, L0_ffn_w_router,
           L0_ffn_corr_bias, L0_ffn_gate_w, L0_ffn_up_w, L0_ffn_down_w, L0_ffn_sh_gate_w,
           L0_ffn_sh_up_w, L0_ffn_sh_down_w):
    import concourse.bacc as bacc
    from concourse.bass_utils import run_bass_kernel_spmd

    c = np.asarray(ctx_2048).reshape(NG, GB, HD, BLK, P).transpose(0, 4, 3, 2, 1)
    gu = np.stack([np.asarray(L0_ffn_gate_w), np.asarray(L0_ffn_up_w)], axis=2)
    gu = gu.reshape(E, KC, P, 2 * M).transpose(2, 0, 1, 3)
    dn = np.asarray(L0_ffn_down_w).reshape(E, 2, MH, L).transpose(2, 0, 1, 3)
    arrays = {
        "x": np.asarray(x),
        "ctx_t": c.reshape(NG, P, BLK * HD * GB),
        "toeplitz": toeplitz_layout(L0_xattn_ssm_kernel),
        "g_xattn": np.asarray(g_xattn), "g_ffn": np.asarray(g_ffn),
        "skip_d": np.asarray(L0_xattn_D),
        "w_router": np.asarray(L0_ffn_w_router), "corr_bias": np.asarray(L0_ffn_corr_bias),
        "w_gu": gu.reshape(P, E * WGU_E), "w_down": dn.reshape(MH, E * WD_E),
        "sh_gu": np.stack([np.asarray(L0_ffn_sh_gate_w), np.asarray(L0_ffn_sh_up_w)]),
        "sh_down": np.asarray(L0_ffn_sh_down_w),
    }
    arrays = {n: np.ascontiguousarray(a) for n, a in arrays.items()}
    nc = bacc.Bacc("TRN2", target_bir_lowering=False, num_devices=1)
    args = [nc.dram_tensor(n, a.shape, mybir.dt.from_np(a.dtype), kind="ExternalInput").ap()
            for n, a in arrays.items()]
    out = nc.dram_tensor("out", (B, HD, L), mybir.dt.float32, kind="ExternalOutput").ap()
    build(nc, *args, out)
    return run_bass_kernel_spmd(nc, [arrays], core_ids=[0]).results[0]["out"]
```

```python
import numpy as np
import concourse.bass as bass
from concourse import mybir
from contextlib import ExitStack

P = 128
B, HD, L = 16, 128, 256
NH, DH = 16, 8
BLK = L // P
GB = 4
NG = B // GB
HALF = NH // 2
NP = DH * (DH + 1) // 2
PAIR_AT = [sum(DH - k for k in range(d)) for d in range(DH)]
E, TOPK = 32, 6
NGRP, TOPG = 8, 4
EPG = E // NGRP
M = 176
MH = M // 2
SHM = 2 * M
T = B * HD
KC = L // P
NT = T * TOPK // P + E
LIST = T
ROW = L + 1 + E
TOK_AT, SCORE_AT = L, L + 1
EARLY = 15
EPS = 1e-5

WGU_E = KC * 2 * M
WD_E = 2 * L
WD_AT = E * WGU_E
ARENA = WD_AT + E * WD_E
CTX_AT = EARLY * WGU_E
TOE_AT = CTX_AT + NG * BLK * HD * GB
XN_AT = TOE_AT + NH * L
PROD_AT = XN_AT + GB * L
PROD_H = BLK * HALF * NP * GB
CONV_AT = PROD_AT + 2 * PROD_H
CONV_H = HALF * BLK * NP * GB
Z_AT = CONV_AT + 2 * CONV_H
Z_SIZE = HALF * BLK * DH * DH * GB
TMP_AT = Z_AT + Z_SIZE
TMP_SIZE = 2912
WIDE_AT = TMP_AT + TMP_SIZE - 3 * P
X2T_AT = TMP_AT + TMP_SIZE
SILU_AT = X2T_AT + GB * L
HS_AT = SILU_AT + SHM
HST_AT = HS_AT + SHM
SHOUT_AT = HST_AT + 4 * P
ROUTER_AT = SHOUT_AT + 2 * L
assert ROUTER_AT + KC * E <= ARENA
STATS_AT, MOMENTS_AT, NEWTON_AT = TMP_AT, TMP_AT + 6 * B, TMP_AT + 8 * B
WD_MID = (TMP_AT - WD_AT) // WD_E
assert WD_AT <= TMP_AT

WORK = BLK * 4 * GB * P
NX = 4
XT_AT = NX * ROW
SG_AT = XT_AT + 2 * L
H_AT = SG_AT + 2 * M
HT_AT = H_AT + 2 * M
Y_AT = HT_AT + 2 * L
TW_AT = Y_AT + NX * L
assert TW_AT + NX <= WORK


def build(nc, x, ctx_t, toeplitz, g_xattn, g_ffn, skip_d, w_router, corr_bias,
          w_gu, w_down, sh_gu, sh_down, out):
    fp32, bf16, u32, i32 = mybir.dt.float32, mybir.dt.bfloat16, mybir.dt.uint32, mybir.dt.int32
    ALU = mybir.AluOpType
    ACT = mybir.ActivationFunctionType
    AX = mybir.AxisListType.X

    lists = nc.dram_tensor("expert_lists", ((E + 1) * LIST, ROW), fp32, kind="Internal").ap()
    sums = [nc.dram_tensor(f"token_sums{i}", (T + P, L), fp32, kind="Internal").ap() for i in range(2)]

    ctx = ExitStack()
    with ctx:
        def sb(name, shape, dt=fp32):
            return ctx.enter_context(nc.sbuf_tensor(name, shape, dt))

        def sem(name):
            return ctx.enter_context(nc.semaphore(name))

        arena = sb("arena", [P, ARENA])
        work = sb("work", [P, WORK])
        rows = sb("rows", [P, B, L])
        shgu_sb = sb("shgu_sb", [P, KC, 2 * SHM])
        shd_sb = sb("shd_sb", [MH, 4, L])
        q_sb = sb("q_sb", [P, NH, BLK, DH, GB])
        payload = sb("payload", [P, GB, ROW])
        blank = sb("blank", [P, ROW])
        ident = sb("ident", [P, P])
        bias_sb = sb("bias_sb", [P, E])
        skip_sb = sb("skip_sb", [P, NH])
        gates = sb("gates", [P, 2])
        before_b = sb("before_b", [P, P], bf16)
        ones_b = sb("ones_b", [P, P], bf16)
        mask_b = sb("mask_b", [P, GB, E], bf16)
        seen_b = sb("seen_b", [P, GB + 1, E], bf16)
        lane_dump = sb("lane_dump", [P, 2])
        lane = lane_dump[:, 0:1]
        dump = lane_dump[:, 1:2]
        tok_id = sb("tok_id", [P, B])
        iota_e = sb("iota_e", [P, E])
        list_at = sb("list_at", [P, E])
        tile_at = sb("tile_at", [P, T // P])
        earlier = sb("earlier", [P, NGRP, NGRP])
        slots = sb("slots", [P, GB, DH], u32)
        norm_x = sb("norm_x", [P, 2, B])
        norm = sb("norm", [P, 2, GB])
        tile_row = sb("tile_row", [P, NT], i32)
        tile_exp = sb("tile_exp", [P, NT], i32)
        tile_dump = sb("tile_dump", [P, NT])
        dest = sb("dest", [P, NX], u32)

        bank = [ctx.enter_context(nc.psum_tensor(f"bank{i}", [P, 512], fp32)) for i in range(8)]

        def win(t, at, dims, parts=P):
            return bass.AP(t, at, [[int(np.prod(t.shape[1:])), parts]] + [list(d) for d in dims])

        ctx_v = win(arena, CTX_AT, [[BLK * HD * GB, NG], [HD * GB, BLK], [DH * GB, NH], [1, DH * GB]])
        toe_v = win(arena, TOE_AT, [[L, NH], [1, L]])
        router_sb = win(arena, ROUTER_AT, [[E, KC], [1, E]])
        stats = win(arena, STATS_AT, [[6, B], [1, 6]])
        moments = win(arena, MOMENTS_AT, [[2, B], [1, 2]])
        newton = win(arena, NEWTON_AT, [[B, 3], [1, B]])
        wgu_v = win(arena, 0, [[1, E * WGU_E]])
        wd_v = win(arena, WD_AT, [[1, E * WD_E]], parts=MH)

        first_in, toe_in, rest_in = sem("first_in"), sem("toe_in"), sem("rest_in")
        consts_done = sem("consts_done")
        iota_done = sem("iota_done")
        toe_done = sem("toe_done")
        tanh_done = sem("tanh_done")
        blank_done = sem("blank_done")
        blanks_stored = sem("blanks_stored")
        table_steps = sem("table_steps")
        norm_others_done = sem("norm_others_done")
        vstep = sem("vector_steps")
        norm_x_done, norm_done, xn_ready, qT_ready, q_ready = sem("norm_x_done"), sem("norm_done"), sem("xn_ready"), sem("qT_ready"), sem("q_ready")
        products_ready, conv_ready, conv_copied = sem("products_ready"), sem("conv_ready"), sem("conv_copied")
        pairs_summed, attn_ready = sem("pairs_summed"), sem("attn_ready")
        x2_ready, x2T_ready, x2T_copied = sem("x2_ready"), sem("x2T_ready"), sem("x2T_copied")
        logits_ready, scores_ready = sem("logits_ready"), sem("scores_ready")
        mask_ready, rank_ready, slots_ready = sem("mask_ready"), sem("rank_ready"), sem("slots_ready")
        scattered, payload_free, shared_free = sem("scattered"), sem("payload_free"), sem("shared_free")
        gate_ready, silu_ready, sh_h_ready = sem("gate_ready"), sem("silu_ready"), sem("sh_h_ready")
        sh_hT_ready, sh_hT_copied = sem("sh_hT_ready"), sem("sh_hT_copied")
        sh_ready, sh_copied, sh_stored = sem("sh_ready"), sem("sh_copied"), sem("sh_stored")
        counts_ready, meta_ready, meta_spread, tables_ready = (
            sem("counts_ready"), sem("meta_ready"), sem("meta_spread"), sem("tables_ready"))
        early_in, late_in = sem("early_weights_in"), sem("late_weights_in")
        t_loaded = [sem(f"tile_loaded{i}") for i in range(NX)]
        t_xT, t_xT_copied, t_gu, t_silu, t_h = sem("t_xT"), sem("t_xT_copied"), sem("t_gu"), sem("t_silu"), sem("t_h")
        t_hT, t_hT_copied, t_y, t_y_copied = sem("t_hT"), sem("t_hT_copied"), sem("t_y"), sem("t_y_copied")
        t_wstep = sem("t_weight_steps")
        t_added = [sem(f"tile_added{i}") for i in range(2)]
        sums_in = [sem(f"sums_in{i}") for i in range(NG)]
        f_added, f_done = sem("final_added"), sem("final_done")
        out_stored = sem("out_stored")

        ctx.enter_context(nc.allow_low_precision(reason="small whole numbers, exact in bfloat16"))
        held = sem("held")

        block = ctx.enter_context(nc.Block())

        def added(t, u):
            return (t // 2 + 1) * 16 if isinstance(t, int) else (t - u % 2) * 8 + 16

        FIRST_IN, REST_IN = 16 * 4, 16 * 7
        V_FIRST, V_LOOP = 28, 40

        @block.sync
        def _(sp):
            x_v = x.rearrange("b p l -> p b l")
            CG = BLK * HD * GB
            sp.dma_start(rows[:, 0:GB, :], x_v[:, 0:GB, :]).then_inc(first_in, 16)
            sp.dma_start(win(arena, CTX_AT, [[1, CG]]), ctx_t[0]).then_inc(first_in, 16)
            sp.dma_start(gates[:, 0:1], g_xattn.partition_broadcast(P)).then_inc(first_in, 16)
            sp.dma_start(gates[:, 1:2], g_ffn.partition_broadcast(P)).then_inc(first_in, 16)
            sp.dma_start(skip_sb[:, :], skip_d.partition_broadcast(P)).then_inc(toe_in, 16)
            sp.dma_start(toe_v, toeplitz).then_inc(toe_in, 16)
            sp.dma_start(rows[:, GB:B, :], x_v[:, GB:B, :]).then_inc(rest_in, 16)
            sp.dma_start(win(arena, CTX_AT + CG, [[CG, NG - 1], [1, CG]]),
                         ctx_t[1:NG].rearrange("g p n -> p g n")).then_inc(rest_in, 16)
            sp.dma_start(bias_sb[:, :], corr_bias.partition_broadcast(P)).then_inc(rest_in, 16)
            sp.dma_start(router_sb[:, :, :], w_router.rearrange("(c p) e -> p c e", p=P)).then_inc(rest_in, 16)
            sp.dma_start(shgu_sb[:, :, 0:SHM], sh_gu[0].rearrange("(c p) m -> p c m", p=P)).then_inc(rest_in, 16)
            sp.dma_start(shgu_sb[:, :, SHM:2 * SHM], sh_gu[1].rearrange("(c p) m -> p c m", p=P)).then_inc(rest_in, 16)
            sp.dma_start(shd_sb[:, :, :], sh_down.rearrange("(c p) n -> p c n", p=MH)).then_inc(rest_in, 16)
            sp.wait_ge(blank_done, 1)
            sp.dma_start(bass.AP(lists.tensor, 0, [[ROW, P], [LIST * ROW, E + 1], [1, ROW]]),
                         win(blank, 0, [[0, E + 1], [1, ROW]])).then_inc(blanks_stored, 16)
            sp.dma_start(sums[1].rearrange("(n p) c -> p n c", p=P),
                         win(blank, 0, [[0, T // P + 1], [1, L]])).then_inc(blanks_stored, 16)
            sp.dma_start(sums[0][T:T + P, :], blank[:, 0:L]).then_inc(blanks_stored, 16)
            sp.dma_start(win(arena, 0, [[1, EARLY * WGU_E]]), w_gu[:, 0:EARLY * WGU_E]).then_inc(early_in, 16)
            sp.sem_inc(shared_free, 2)
            def store_shared(g):
                for b in range(GB):
                    sp.wait_ge(sh_copied, g * GB + b + 1)
                    sp.dma_start(sums[0].rearrange("(n p) c -> p n c", p=P)[:, bass.ds(g * GB + b, 1), :],
                                 win(arena, SHOUT_AT + b % 2 * L, [[L, 1], [1, L]])).then_inc(sh_stored, 16)
                    sp.wait_ge(sh_stored, g * (GB * 16) + (b + 1) * 16)
                    sp.sem_inc(shared_free, 1)

            with sp.Fori(0, NG - 1) as g:
                store_shared(g)
            store_shared(NG - 1)
            sp.wait_ge(tables_ready, 1)
            sp.dma_start(wd_v[:, WD_MID * WD_E:E * WD_E], w_down[:, WD_MID * WD_E:E * WD_E]).then_inc(late_in, 16)
            sp.wait_ge(t_added[0], 16 * (NT // 2))
            sp.wait_ge(t_added[1], 16 * (NT // 2))
            for c in range(NG):
                for i in range(2):
                    sp.dma_start(win(arena, (2 * c + i) * GB * L, [[L, GB], [1, L]]),
                                 sums[i].rearrange("(n p) c -> p n c", p=P)[:, c * GB:(c + 1) * GB, :]
                                 ).then_inc(sums_in[c], 16)
            for c in range(NG):
                sp.wait_ge(f_done, c + 1)
                sp.dma_start(out.rearrange("b p l -> p b l")[:, c * GB:(c + 1) * GB, :],
                             win(arena, 2 * c * GB * L, [[L, GB], [1, L]])).then_inc(out_stored, 16)
            sp.wait_ge(out_stored, 16 * NG)

        @block.gpsimd
        def _(pool):
            step = [0]

            def link(ins):
                step[0] += 1
                ins.then_inc(iota_done, 1)
                pool.wait_ge(iota_done, step[0])

            iota_i = win(work, 0, [[1, 1 + E]]).bitcast(i32)
            nc.gpsimd.memset(ident[:, :], 0.0)
            nc.gpsimd.memset(before_b[:, :], 0.0)
            nc.gpsimd.memset(ones_b[:, :], 1.0)
            nc.gpsimd.memset(seen_b[:, :, :], 0.0)
            link(nc.gpsimd.memset(earlier[:, :, :], 0.0))
            nc.gpsimd.affine_select(out=ident[:, :], in_=ident[:, :], compare_op=ALU.not_equal, fill=1.0,
                                    base=0, pattern=[[-1, P]], channel_multiplier=1)
            nc.gpsimd.affine_select(out=before_b[:, :], in_=before_b[:, :], compare_op=ALU.is_ge, fill=1.0,
                                    base=0, pattern=[[-1, P]], channel_multiplier=1)
            nc.gpsimd.affine_select(out=earlier[:, :, :], in_=earlier[:, :, :], compare_op=ALU.is_ge, fill=1.0,
                                    base=0, pattern=[[-1, NGRP], [1, NGRP]], channel_multiplier=0)
            nc.gpsimd.iota(iota_i[:, 0:1], pattern=[[0, 1]], base=0, channel_multiplier=1)
            link(nc.gpsimd.iota(iota_i[:, 1:33], pattern=[[1, E]], base=0, channel_multiplier=0))
            nc.gpsimd.tensor_copy(lane[:, :], iota_i[:, 0:1])
            link(nc.gpsimd.tensor_copy(iota_e[:, :], iota_i[:, 1:33]))
            nc.gpsimd.tensor_scalar(dump[:, :], lane[:, :], float(T), None, ALU.add)
            nc.gpsimd.tensor_scalar(list_at[:, :], iota_e[:, :], float(LIST), None, ALU.mult)
            link(nc.gpsimd.tensor_scalar(tile_at[:, :], iota_e[:, 0:T // P], float(P), None, ALU.mult))
            link(nc.gpsimd.tensor_scalar(tok_id[:, :], tile_at[:, :], lane[:, 0:1], None, ALU.add))
            nc.gpsimd.memset(blank[:, :], 0.0).then_inc(consts_done, 1)
            pool.wait_ge(consts_done, 1)
            nc.gpsimd.tensor_copy(blank[:, TOK_AT:TOK_AT + 1], dump[:, :]).then_inc(blank_done, 1)

            pool.wait_ge(blanks_stored, 48)
            pool.sem_inc(payload_free, 1)
            with pool.Fori(0, NG) as g:
                pool.wait_ge(slots_ready, g + 1)
                pool.sem_inc(held, 1)
                for b in range(GB):
                    for k in range(TOPK):
                        nc.gpsimd.indirect_dma_start(
                            lists, bass.IndirectOffsetOnAxis(ap=slots[:, b, k:k + 1], axis=0),
                            payload[:, b, :], None).then_inc(scattered, 16)
                pool.wait_ge(scattered, (g + 1) * (GB * TOPK * 16))
                pool.sem_inc(payload_free, 1)

            def add_tile(t, u):
                pool.wait_ge(t_y_copied, t + 1)
                pool.wait_ge(t_wstep, t + 1)
                if not (isinstance(t, int) and t < 2):
                    pool.wait_ge(t_added[u % 2], added(t - 2, u))
                pool.sem_inc(held, 1)
                nc.gpsimd.indirect_dma_start(
                    sums[u % 2], bass.IndirectOffsetOnAxis(ap=dest[:, u:u + 1], axis=0),
                    win(work, Y_AT + u * L, [[1, L]]), None,
                    compute_op=ALU.add).then_inc(t_added[u % 2], 16)

            pool.wait_ge(sh_stored, 16 * B)
            for t in range(4):
                add_tile(t, t % 4)
            with pool.Fori(1, NT // 4) as n:
                for u in range(4):
                    add_tile(n * 4 + u, u)

        @block.scalar
        def _(act):
            act.wait_ge(first_in, FIRST_IN)
            nc.scalar.activation(gates[:, :], gates[:, :], ACT.Tanh).then_inc(tanh_done, 1)

            def group(g, attend, route):

                def empty_conv(s):
                    for h in range(s * HALF, (s + 1) * HALF):
                        act.wait_ge(conv_ready, (g + 1) * NH + h + 1)
                        nc.scalar.copy(win(arena, CONV_AT + h * BLK * NP * GB, [[1, BLK * NP * GB]]),
                                       bank[2 + h % 2][:, 0:BLK * NP * GB]).then_inc(conv_copied, 1)

                def silu(b):
                    act.wait_ge(gate_ready, g * GB + b + 1)
                    nc.scalar.activation(win(arena, SILU_AT, [[1, SHM]]), bank[5][:, 0:SHM], ACT.Silu).then_inc(silu_ready, 1)

                def copy_sh_hT(b):
                    act.wait_ge(sh_hT_ready, g * GB + b + 1)
                    nc.scalar.copy(win(arena, HST_AT, [[1, 512]], parts=MH), bank[7][0:MH, :]).then_inc(sh_hT_copied, 1)

                def copy_shared(b):
                    act.wait_ge(shared_free, g * GB + b + 1)
                    act.wait_ge(sh_ready, g * GB + b + 1)
                    nc.scalar.copy(win(arena, SHOUT_AT + b % 2 * L, [[1, L]]), bank[4][:, 0:L]).then_inc(sh_copied, 1)

                if attend:
                    if route:
                        act.wait_ge(norm_others_done, 1)
                    else:
                        act.wait_ge(norm_x_done, 1)
                    for b in range(GB):
                        scale, bias = (norm_x[:, i, bass.ds((g + 1) * GB + b, 1)] for i in range(2))
                        last = nc.scalar.activation(win(arena, XN_AT + b * L, [[1, L]]), rows[:, bass.ds((g + 1) * GB + b, 1), :],
                                                    ACT.Identity, bias=bias, scale=scale)
                    last.then_inc(xn_ready, 1)
                    for p in range(2):
                        act.wait_ge(qT_ready, (g + 1) * 2 + p + 1)
                        for b in range(2):
                            last = nc.scalar.copy(
                                win(q_sb, 2 * p + b, [[DH * GB, BLK], [BLK * DH * GB, NH], [GB, DH]]),
                                win(bank[5 + p], b * L, [[P, BLK], [DH, NH], [1, DH]]))
                        last.then_inc(q_ready, 1)
                    empty_conv(0)
                if route:
                    act.wait_ge(norm_done, g + 1)
                    act.wait_ge(payload_free, g + 1)
                    act.sem_inc(held, 1)
                    for b in range(GB):
                        last = nc.scalar.activation(payload[:, b, 0:L], rows[:, bass.ds(g * GB + b, 1), :],
                                                    ACT.Identity, bias=norm[:, 1, b:b + 1], scale=norm[:, 0, b:b + 1])
                    last.then_inc(x2_ready, 1)
                    if not attend:
                        act.wait_ge(pairs_summed, 2 * NG)
                        act.dma_start(win(arena, EARLY * WGU_E, [[1, (E - EARLY) * WGU_E]]),
                                      w_gu[:, EARLY * WGU_E:E * WGU_E]).then_inc(late_in, 16)
                        act.dma_start(wd_v[:, 0:WD_MID * WD_E], w_down[:, 0:WD_MID * WD_E]).then_inc(late_in, 16)
                    for p in range(2):
                        act.wait_ge(x2T_ready, g * 2 + p + 1)
                        nc.scalar.copy(win(arena, X2T_AT + p * 512, [[1, 512]]), bank[p][:, :]).then_inc(x2T_copied, 1)
                if route:
                    act.wait_ge(logits_ready, g + 1)
                    nc.scalar.activation(payload[:, :, SCORE_AT:ROW], win(bank[4], 0, [[E, GB], [1, E]]),
                                         ACT.Sigmoid).then_inc(scores_ready, 1)
                    silu(0)
                if attend:
                    empty_conv(1)
                if route:
                    for b in range(GB):
                        copy_sh_hT(b)
                        if b + 1 < GB:
                            silu(b + 1)
                        copy_shared(b)

            group(-1, True, False)
            with act.Fori(0, NG - 1) as g:
                group(g, True, True)
            group(NG - 1, False, True)

            act.wait_ge(tables_ready, 1)
            act.wait_ge(payload_free, NG + 1)

            def load_tile(t, u):
                first = act.value_load(tile_row[0:1, bass.ds(t, 1)], min_val=0, max_val=E * LIST)
                if not (isinstance(t, int) and t < NX):
                    act.wait_ge(t_wstep, t - NX + 1)
                    act.wait_ge(t_xT, t - NX + 1)
                act.dma_start(win(work, u * ROW, [[1, ROW]]), lists[bass.ds(first, P), :]).then_inc(t_loaded[u], 16)

            def copy_xT(t, u):
                act.wait_ge(t_xT, t + 1)
                nc.scalar.copy(win(work, XT_AT + u % 2 * L, [[1, L]]), bank[u % 2][:, 0:L]).then_inc(t_xT_copied, 1)

            def silu(t, u):
                act.wait_ge(t_gu, t + 1)
                nc.scalar.activation(win(work, SG_AT + u % 2 * M, [[1, M]]), bank[2 + u % 2][:, 0:M],
                                     ACT.Silu).then_inc(t_silu, 1)

            def copy_y(t, u):
                act.wait_ge(t_y, t + 1)
                if not (isinstance(t, int) and t < NX):
                    act.wait_ge(t_added[u % 2], added(t - NX, u))
                nc.scalar.copy(win(work, Y_AT + u * L, [[1, L]]), bank[6 + u % 2][:, 0:L]).then_inc(t_y_copied, 1)

            def tile_step(t, u, lo=0, hi=NT):
                if not isinstance(t, int) or t + 1 < NT:
                    copy_xT(t + 1, (u + 1) % 4)
                if not isinstance(t, int) or t + 3 < NT and t >= 1:
                    load_tile(t + 3, (u + 3) % 4)
                if not isinstance(t, int) or t < NT:
                    silu(t, u)
                if not isinstance(t, int) or t >= 2:
                    copy_y(t - 2, (u + 2) % 4)

            for t in range(4):
                load_tile(t, t)
            copy_xT(0, 0)
            for t in range(4):
                tile_step(t, t)
            with act.Fori(1, NT // 4 - 1) as n:
                for u in range(4):
                    tile_step(n * 4 + u, u)
            for t in range(NT - 4, NT + 2):
                tile_step(t, t % 4)

        @block.vector
        def _(dve):
            count = [0]

            def group(g, attend, route, start):
                count[0] = 0

                def link(ins, hold=False):
                    count[0] += 1
                    ins.then_inc(vstep, 1)
                    dve.wait_ge(vstep, start + count[0])
                    if hold:
                        dve.sem_inc(held, 1)

                def layernorms(row, n, r, done):
                    for b in range(n):
                        last = nc.vector.bn_stats(stats[:, b, :], rows[:, bass.ds(row + b, 1), :].rearrange("p a l -> p (a l)"))
                    link(last, hold=True)
                    for b in range(n):
                        last = nc.vector.bn_aggr(moments[:, b, :], stats[:, b, :])
                    link(last)
                    v, y, z = (newton[:, i, 0:n] for i in range(3))
                    link(nc.vector.tensor_scalar(v, moments[:, 0:n, 1], EPS, None, ALU.add))
                    link(nc.vector.tensor_scalar(y.bitcast(i32), v.bitcast(i32), -0.5, float(0x5F3759DF),
                                                 ALU.mult, ALU.add))
                    for i in range(3):
                        link(nc.vector.tensor_tensor(z, y, y, ALU.mult))
                        link(nc.vector.scalar_tensor_tensor(z, z, -0.5, v, ALU.mult, ALU.mult))
                        link(nc.vector.scalar_tensor_tensor(r[:, 0, :] if i == 2 else y, z, 1.5, y, ALU.add, ALU.mult))
                    nc.vector.scalar_tensor_tensor(r[:, 1, :], moments[:, 0:n, 0], -1.0, r[:, 0, :],
                                                   ALU.mult, ALU.mult).then_inc(done, 1)

                def products():
                    for s in range(2):
                        for d in range(DH):
                            n = (DH - d) * GB
                            c = ctx_v[:, bass.ds(g + 1, 1), :, s * HALF:(s + 1) * HALF, :].rearrange("p a k h n -> p (a k) h n")
                            last = nc.vector.tensor_tensor(
                                win(arena, PROD_AT + s * PROD_H + PAIR_AT[d] * GB,
                                    [[HALF * NP * GB, BLK], [NP * GB, HALF], [1, n]]),
                                c[:, :, :, 0:n], c[:, :, :, d * GB:d * GB + n], ALU.mult)
                        last.then_inc(products_ready, 1)

                HB = HALF * BLK

                def times_q(s):
                    dve.wait_ge(conv_copied, (g + 1) * NH + (s + 1) * HALF)
                    if s == 0:
                        dve.wait_ge(q_ready, (g + 1) * 2 + 2)
                    for d in range(DH):
                        y = win(arena, CONV_AT + s * CONV_H + PAIR_AT[d] * GB, [[NP * GB, HB], [GB, DH - d], [1, GB]])
                        for i0, z0 in ((0, d * GB), (d, d * DH * GB)) if d else ((0, 0),):
                            last = nc.vector.tensor_tensor(
                                win(arena, Z_AT + z0, [[DH * DH * GB, HB], [(DH + 1) * GB, DH - d], [1, GB]]),
                                y, win(q_sb, s * HB * DH * GB + i0 * GB, [[DH * GB, HB], [GB, DH - d], [1, GB]]),
                                ALU.mult)
                    link(last)

                def sum_pairs(s):
                    ZH = DH * DH * GB
                    for k in range(BLK):
                        for i in range(4):
                            z = [win(arena, Z_AT + k * ZH + ii * DH * GB, [[BLK * ZH, HALF], [GB, DH], [1, GB]])
                                 for ii in (i, i + 4)]
                            last = nc.vector.tensor_tensor(
                                win(work, (k * 4 + i) * GB * P + s * HALF * DH, [[DH, HALF], [1, DH], [P, GB]]),
                                z[0], z[1], ALU.add)
                    last.then_inc(pairs_summed, 1)
                    dve.wait_ge(pairs_summed, (g + 1) * 2 + s + 1)

                def shared_times(b):
                    dve.wait_ge(silu_ready, g * GB + b + 1)
                    if b:
                        dve.wait_ge(sh_hT_ready, g * GB + b)
                    nc.vector.tensor_tensor(win(arena, HS_AT, [[1, SHM]]), win(arena, SILU_AT, [[1, SHM]]),
                                            bank[6][:, 0:SHM], ALU.mult).then_inc(sh_h_ready, 1)

                def choose():
                    dve.wait_ge(scores_ready, g + 1)
                    nc.vector.tensor_copy(payload[:, :, TOK_AT], tok_id[:, bass.ds(g * GB, GB)])
                    at = [TMP_AT]

                    def tmp(*shape):
                        n = int(np.prod(shape))
                        o = at[0]
                        at[0] += n
                        return o

                    def flat(o, n, step=1):
                        return win(arena, o, [[step, n]])

                    scores = payload[:, :, SCORE_AT:ROW]
                    sfc = tmp(GB, E)
                    link(nc.vector.tensor_tensor(win(arena, sfc, [[E, GB], [1, E]]), scores,
                                                 win(bias_sb, 0, [[0, GB], [1, E]]), ALU.add))
                    NP2 = GB * E // 2
                    hi2, lo2 = tmp(NP2), tmp(NP2)
                    nc.vector.tensor_tensor(flat(hi2, NP2), flat(sfc, NP2, 2), flat(sfc + 1, NP2, 2), ALU.max)
                    link(nc.vector.tensor_tensor(flat(lo2, NP2), flat(sfc, NP2, 2), flat(sfc + 1, NP2, 2), ALU.min))
                    G4 = GB * NGRP
                    best, a2, c2, gs = tmp(G4), tmp(G4), tmp(G4), tmp(G4)
                    nc.vector.tensor_tensor(flat(best, G4), flat(hi2, G4, 2), flat(hi2 + 1, G4, 2), ALU.max)
                    nc.vector.tensor_tensor(flat(a2, G4), flat(hi2, G4, 2), flat(hi2 + 1, G4, 2), ALU.min)
                    link(nc.vector.tensor_tensor(flat(c2, G4), flat(lo2, G4, 2), flat(lo2 + 1, G4, 2), ALU.max))
                    link(nc.vector.tensor_tensor(flat(a2, G4), flat(a2, G4), flat(c2, G4), ALU.max))
                    link(nc.vector.tensor_tensor(flat(gs, G4), flat(best, G4), flat(a2, G4), ALU.add))
                    cmp, eq = tmp(GB, NGRP, NGRP), tmp(GB, NGRP, NGRP)
                    dims = [[NGRP * NGRP, GB], [NGRP, NGRP], [1, NGRP]]
                    other = win(arena, gs, [[NGRP, GB], [0, NGRP], [1, NGRP]])
                    own = win(arena, gs, [[NGRP, GB], [1, NGRP], [0, NGRP]])
                    nc.vector.tensor_tensor(win(arena, cmp, dims), other, own, ALU.is_gt)
                    link(nc.vector.tensor_tensor(win(arena, eq, dims), other, own, ALU.is_equal))
                    link(nc.vector.tensor_tensor(win(arena, eq, dims), win(arena, eq, dims),
                                                 win(earlier, 0, [[0, GB], [NGRP, NGRP], [1, NGRP]]), ALU.mult))
                    link(nc.vector.tensor_tensor(flat(cmp, GB * 64), flat(cmp, GB * 64), flat(eq, GB * 64), ALU.add))
                    grank, keep, off = tmp(G4), tmp(G4), tmp(G4)
                    link(nc.vector.tensor_reduce(flat(grank, G4), win(arena, cmp, [[NGRP, G4], [1, NGRP]]), AX, ALU.add))
                    link(nc.vector.tensor_scalar(flat(keep, G4), flat(grank, G4), float(TOPG), None, ALU.is_lt))
                    link(nc.vector.tensor_scalar(flat(off, G4), flat(keep, G4), -1.0, 1e30, ALU.add, ALU.mult))
                    each = lambda o: win(arena, o, [[1, G4], [0, EPG]])
                    four = lambda o: win(arena, o, [[EPG, G4], [1, EPG]])
                    masked = tmp(GB, E)
                    link(nc.vector.tensor_tensor(four(masked), four(sfc), each(keep), ALU.mult))
                    link(nc.vector.tensor_tensor(four(masked), four(masked), each(off), ALU.add), hold=True)
                    top, top_i, top_f = tmp(GB, 8), tmp(GB, 8), tmp(GB, 8)
                    idx = lambda o, n: win(arena, o, [[1, n]]).bitcast(u32)
                    for b in range(GB):
                        last = nc.vector.max(flat(top + 8 * b, 8), flat(masked + E * b, E))
                    link(last, hold=True)
                    for b in range(GB):
                        last = nc.vector.max_index(idx(top_i + 8 * b, 8), flat(top + 8 * b, 8), flat(masked + E * b, E))
                    link(last)
                    link(nc.vector.tensor_copy(flat(top_f, 8 * GB), idx(top_i, 8 * GB)))
                    onehot, part = tmp(GB, TOPK, E), tmp(GB, TOPK, E)
                    bke = [[TOPK * E, GB], [E, TOPK], [1, E]]
                    link(nc.vector.tensor_tensor(win(arena, onehot, bke), win(iota_e, 0, [[0, GB], [0, TOPK], [1, E]]),
                                                 win(arena, top_f, [[8, GB], [1, TOPK], [0, E]]), ALU.is_equal))
                    link(nc.vector.tensor_reduce(mask_b[:, :, :], win(arena, onehot, [[TOPK * E, GB], [1, E], [E, TOPK]]),
                                                 AX, ALU.add))
                    for b in range(GB):
                        ins = nc.vector.tensor_tensor(seen_b[:, b + 1, :], seen_b[:, b, :], mask_b[:, b, :], ALU.add)
                        link(ins) if b + 1 < GB else ins.then_inc(mask_ready, 1)
                    return onehot, part, bke, tmp

                def place_rows(onehot, part, bke, tmp):
                    dve.wait_ge(mask_ready, g + 1)
                    dve.wait_ge(rank_ready, g + 1)
                    nc.vector.tensor_copy(seen_b[:, 0, :], seen_b[:, GB, :])
                    place = tmp(GB, E)
                    link(nc.vector.tensor_tensor(win(arena, place, [[E, GB], [1, E]]), win(bank[4], GB * E, [[E, GB], [1, E]]),
                                                 win(list_at, 0, [[0, GB], [1, E]]), ALU.add))
                    link(nc.vector.tensor_tensor(win(arena, part, bke), win(arena, onehot, bke),
                                                 win(arena, place, [[E, GB], [0, TOPK], [1, E]]), ALU.mult))
                    slot_f = tmp(GB, TOPK)
                    link(nc.vector.tensor_reduce(win(arena, slot_f, [[1, GB * TOPK]]), win(arena, part, [[E, GB * TOPK], [1, E]]),
                                                 AX, ALU.add))
                    nc.vector.tensor_copy(slots[:, :, 0:TOPK], win(arena, slot_f, [[TOPK, GB], [1, TOPK]])).then_inc(slots_ready, 1)

                if not route:
                    layernorms(0, GB, norm_x[:, :, 0:GB], norm_x_done)
                if attend:
                    products()
                if route:
                    for p in range(2):
                        dve.wait_ge(attn_ready, g * 2 + p + 1)
                        r = rows[:, bass.ds(g * GB + 2 * p, 2), :].rearrange("p b l -> p (b l)")
                        last = nc.vector.scalar_tensor_tensor(r, bank[p][:, :], gates[:, 0:1], r, ALU.mult, ALU.add)
                    link(last, hold=True)
                    layernorms(g * GB, GB, norm, norm_done)
                else:
                    dve.wait_ge(toe_in, 32)
                    for h in range(NH):
                        diag = win(arena, TOE_AT + h * L, [[1, P]])
                        last = nc.vector.scalar_tensor_tensor(diag, ident[:, :], skip_sb[:, h:h + 1], diag, ALU.mult, ALU.add)
                    last.then_inc(toe_done, 1)
                    dve.wait_ge(rest_in, REST_IN)
                    dve.wait_ge(norm_x_done, 1)
                    layernorms(GB, B - GB, norm_x[:, :, GB:B], norm_others_done)
                if attend:
                    times_q(0)
                if route:
                    shared_times(0)
                    chosen = choose()
                if attend:
                    sum_pairs(0)
                if route:
                    place_rows(*chosen)
                    if not attend:
                        describe_tiles()
                    shared_times(1)
                if attend:
                    times_q(1)
                if route:
                    shared_times(2)
                if attend:
                    sum_pairs(1)
                if route:
                    shared_times(3)
                return count[0]

            def describe_tiles():
                base = [0]

                def chain(ins):
                    base[0] += 1
                    ins.then_inc(table_steps, 1)
                    dve.wait_ge(table_steps, base[0])

                at = [TMP_AT]

                def tmp(n):
                    at[0] += n
                    return at[0] - n

                def flat(o, n=1):
                    return win(arena, o, [[1, n]])

                cnt, cmp, nt = tmp(E), tmp(E * (T // P)), tmp(E)
                PAD = E // 2
                run = [tmp(PAD + E), tmp(PAD + E)]
                nc.vector.memset(flat(run[0], PAD), 0.0)
                nc.vector.memset(flat(run[1], PAD), 0.0)
                dve.wait_ge(counts_ready, 1)
                chain(nc.vector.tensor_copy(flat(cnt, E), bank[0][:, 0:E]))
                chain(nc.vector.tensor_tensor(win(arena, cmp, [[T // P, E], [1, T // P]]), win(arena, cnt, [[1, E], [0, T // P]]),
                                              win(tile_at, 0, [[0, E], [1, T // P]]), ALU.is_gt))
                chain(nc.vector.tensor_reduce(flat(nt, E), win(arena, cmp, [[T // P, E], [1, T // P]]), AX, ALU.add))
                chain(nc.vector.tensor_copy(flat(run[0] + PAD, E), flat(nt, E)))
                s, src = 1, 0
                while s < E:
                    chain(nc.vector.tensor_tensor(flat(run[1 - src] + PAD, E), flat(run[src] + PAD, E),
                                                  flat(run[src] + PAD - s, E), ALU.add))
                    s, src = 2 * s, 1 - src
                past, pn, ex, first, n_e, c1 = tmp(E), tmp(E), tmp(1), tmp(1), tmp(1), tmp(1)
                chain(nc.vector.tensor_scalar(flat(past, E), flat(run[src] + PAD, E), lane[:, 0:1], None, ALU.is_le))
                chain(nc.vector.tensor_tensor(flat(pn, E), flat(past, E), flat(nt, E), ALU.mult))
                nc.vector.tensor_reduce(flat(ex), flat(past, E), AX, ALU.add)
                chain(nc.vector.tensor_reduce(flat(first), flat(pn, E), AX, ALU.add))
                chain(nc.vector.tensor_scalar(flat(past, E), iota_e[:, :], flat(ex), None, ALU.is_equal))
                chain(nc.vector.tensor_tensor(flat(pn, E), flat(past, E), flat(cnt, E), ALU.mult))
                chain(nc.vector.tensor_reduce(flat(n_e), flat(pn, E), AX, ALU.add))
                off, top, start, meta = tmp(1), tmp(1), tmp(1), tmp(3)
                chain(nc.vector.tensor_scalar(flat(off), lane[:, :], flat(first), float(P), ALU.subtract, ALU.mult))
                chain(nc.vector.tensor_scalar(flat(top), flat(n_e), -float(P), 0.0, ALU.add, ALU.max))
                chain(nc.vector.tensor_tensor(flat(start), flat(off), flat(top), ALU.min))
                chain(nc.vector.scalar_tensor_tensor(flat(meta), flat(ex), float(LIST), flat(start), ALU.mult, ALU.add))
                chain(nc.vector.tensor_scalar(flat(meta + 1), flat(ex), float(E - 1), None, ALU.min))
                chain(nc.vector.tensor_tensor(flat(meta + 2), flat(off), flat(start), ALU.subtract))
                assert at[0] <= WIDE_AT
                nc.vector.tensor_copy(win(arena, WIDE_AT, [[P, 3], [1, P]]), win(arena, meta, [[1, 3], [0, P]])).then_inc(meta_ready, 1)
            dve.wait_ge(first_in, FIRST_IN)
            dve.wait_ge(iota_done, 5)
            steps = group(-1, True, False, 0)
            assert steps == V_FIRST, steps
            dve.wait_ge(tanh_done, 1)
            with dve.Fori(0, NG - 1) as g:
                steps = group(g, True, True, g * V_LOOP + V_FIRST)
                assert steps == V_LOOP, steps
            group(NG - 1, False, True, V_FIRST + (NG - 1) * V_LOOP)
            dve.wait_ge(meta_spread, 1)
            nc.vector.tensor_copy(tile_row[:, :], bank[1][:, 0:P])
            nc.vector.tensor_copy(tile_exp[:, :], bank[1][:, P:2 * P])
            nc.vector.tensor_scalar(tile_dump[:, :], bank[1][:, 2 * P:3 * P], lane[:, 0:1], dump[:, 0:1],
                                    ALU.is_gt, ALU.mult).then_inc(tables_ready, 1)

            dve.wait_ge(tables_ready, 1)

            def times(t, u):
                e = dve.value_load(tile_exp[0:1, bass.ds(t, 1)], min_val=0, max_val=E - 1)
                dve.wait_ge(t_loaded[u], (t // 4 + 1) * 16 if isinstance(t, int) else (t - u) * 4 + 16)
                x_at = u * ROW
                w = win(work, TW_AT + u, [[1, 1]])
                nc.vector.tensor_copy(w, win(work, x_at + SCORE_AT, [[1, E]])[:, bass.ds(e, 1)])
                if not (isinstance(t, int) and t < NX):
                    dve.wait_ge(t_added[u % 2], added(t - NX, u))
                nc.vector.tensor_tensor(dest[:, u:u + 1], win(work, x_at + TOK_AT, [[1, 1]]),
                                        tile_dump[:, bass.ds(t, 1)], ALU.max).then_inc(t_wstep, 1)
                dve.wait_ge(t_wstep, t + 1)
                dve.wait_ge(t_silu, t + 1)
                nc.vector.scalar_tensor_tensor(win(work, H_AT + u % 2 * M, [[1, M]]), win(work, SG_AT + u % 2 * M, [[1, M]]),
                                               w, bank[2 + u % 2][:, M:2 * M], ALU.mult, ALU.mult).then_inc(t_h, 1)

            def copy_hT(t, u):
                dve.wait_ge(t_hT, t + 1)
                nc.vector.tensor_copy(win(work, HT_AT + u % 2 * L, [[1, L]], parts=MH),
                                      bank[4 + u % 2][0:MH, 0:L]).then_inc(t_hT_copied, 1)

            def tile_step(t, u):
                if not isinstance(t, int) or t < NT:
                    times(t, u)
                if not isinstance(t, int) or 1 <= t <= NT:
                    copy_hT(t - 1, (u + 3) % 4)

            for t in range(4):
                tile_step(t, t)
            with dve.Fori(1, NT // 4 - 1) as n:
                for u in range(4):
                    tile_step(n * 4 + u, u)
            for t in range(NT - 4, NT + 1):
                tile_step(t, t % 4)

            for c in range(NG):
                a = win(arena, 2 * c * GB * L, [[1, GB * L]])
                b = win(arena, (2 * c + 1) * GB * L, [[1, GB * L]])
                dve.wait_ge(sums_in[c], 32)
                nc.vector.tensor_tensor(a, a, b, ALU.add).then_inc(f_added, 1)
                dve.wait_ge(f_added, c + 1)
                nc.vector.scalar_tensor_tensor(a, a, gates[:, 1:2],
                                               rows[:, c * GB:(c + 1) * GB, :].rearrange("p b l -> p (b l)"),
                                               ALU.mult, ALU.add).then_inc(f_done, 1)

        @block.tensor
        def _(pe):
            prods = lambda s, h, k, n: win(arena, PROD_AT + s * PROD_H + (k * HALF + h) * NP * GB,
                                           [[HALF * NP * GB, n], [1, NP * GB]])
            toe = lambda h, a: win(arena, TOE_AT + h * L + a * P, [[1, P]])
            x2T = lambda b, k: win(arena, X2T_AT + (b * KC + k) * P, [[1, P]])
            CB = NP * GB

            def group(g, attend, route):

                def convolve(s):
                    pe.wait_ge(products_ready, (g + 1) * 2 + s + 1)
                    for hh in range(HALF):
                        h = s * HALF + hh
                        if h >= 2:
                            pe.wait_ge(conv_copied, (g + 1) * NH + h - 1)
                        y = bank[2 + h % 2]
                        nc.tensor.matmul(y[:, 0:2 * CB], toe(h, 0), prods(s, hh, 0, 2), start=True, stop=False)
                        nc.tensor.matmul(y[:, CB:2 * CB], toe(h, 1), prods(s, hh, 0, 1), start=False,
                                         stop=True).then_inc(conv_ready, 1)

                def attention():
                    pe.wait_ge(pairs_summed, g * 2 + 2)
                    for p in range(2):
                        for b in range(2):
                            for k in range(BLK):
                                for i in range(4):
                                    last = nc.tensor.matmul(
                                        bank[p][:, (b * BLK + k) * P:(b * BLK + k + 1) * P],
                                        win(work, ((k * 4 + i) * GB + 2 * p + b) * P, [[1, P]]), ident[:, :],
                                        start=(i == 0), stop=(i == 3))
                        last.then_inc(attn_ready, 1)

                def transpose_rows(source, to, ready):
                    for p in range(2):
                        for b in range(2):
                            for k in range(KC):
                                last = nc.tensor.transpose(bank[to + p][:, (b * KC + k) * P:(b * KC + k + 1) * P],
                                                           source(2 * p + b, k), ident[:, :])
                        last.then_inc(ready, 1)

                def shared_up(b):
                    if b:
                        pe.wait_ge(sh_h_ready, g * GB + b)
                    for half in range(2):
                        for k in range(KC):
                            last = nc.tensor.matmul(bank[5 + half][:, 0:SHM], x2T(b, k),
                                                    shgu_sb[:, k, half * SHM:(half + 1) * SHM],
                                                    start=(k == 0), stop=(k == KC - 1))
                    last.then_inc(gate_ready, 1)

                def shared_hT(b):
                    pe.wait_ge(sh_h_ready, g * GB + b + 1)
                    if b:
                        pe.wait_ge(sh_hT_copied, g * GB + b)
                    for c in range(4):
                        last = nc.tensor.transpose(bank[7][0:MH, c * P:(c + 1) * P],
                                                   win(arena, HS_AT + c * MH, [[1, MH]]), ident[:, :])
                    last.then_inc(sh_hT_ready, 1)

                def shared_down(b):
                    pe.wait_ge(sh_hT_copied, g * GB + b + 1)
                    if b:
                        pe.wait_ge(sh_copied, g * GB + b)
                    for c in range(4):
                        last = nc.tensor.matmul(bank[4][:, 0:L], win(arena, HST_AT + c * P, [[1, P]], parts=MH),
                                                shd_sb[:, c, :], start=(c == 0), stop=(c == 3))
                    last.then_inc(sh_ready, 1)

                if route:
                    attention()
                if attend:
                    pe.wait_ge(xn_ready, g + 2)
                    transpose_rows(lambda b, k: win(arena, XN_AT + b * L + k * P, [[1, P]]), 5, qT_ready)
                    convolve(0)
                if route:
                    pe.wait_ge(x2_ready, g + 1)
                    transpose_rows(lambda b, k: payload[:, b, k * P:(k + 1) * P], 0, x2T_ready)
                    pe.wait_ge(x2T_copied, g * 2 + 2)
                    for b in range(GB):
                        for k in range(KC):
                            last = nc.tensor.matmul(bank[4][:, b * E:(b + 1) * E], x2T(b, k), router_sb[:, k, :],
                                                    start=(k == 0), stop=(k == KC - 1))
                    last.then_inc(logits_ready, 1)
                    if attend:
                        pe.wait_ge(q_ready, (g + 1) * 2 + 2)
                    shared_up(0)
                if attend:
                    convolve(1)
                if route:
                    shared_hT(0)
                    pe.wait_ge(mask_ready, g + 1)
                    nc.tensor.matmul(bank[4][:, GB * E:2 * GB * E], before_b[:, :],
                                     mask_b[:, :, :].rearrange("p b e -> p (b e)"), start=True, stop=False)
                    nc.tensor.matmul(bank[4][:, GB * E:2 * GB * E], ones_b[:, :],
                                     seen_b[:, 0:GB, :].rearrange("p b e -> p (b e)"), start=False,
                                     stop=True).then_inc(rank_ready, 1)
                    shared_up(1)
                    pe.wait_ge(slots_ready, g + 1)
                    if not attend:
                        nc.tensor.matmul(bank[0][:, 0:E], ones_b[:, :], seen_b[:, 0, :], start=True,
                                         stop=True).then_inc(counts_ready, 1)
                    for b in range(GB):
                        shared_down(b)
                        if b + 1 < GB:
                            shared_hT(b + 1)
                        if b + 2 < GB:
                            shared_up(b + 2)

            pe.wait_ge(iota_done, 5)
            pe.wait_ge(toe_done, 1)
            group(-1, True, False)
            pe.wait_ge(rest_in, REST_IN)
            with pe.Fori(0, NG - 1) as g:
                group(g, True, True)
            group(NG - 1, False, True)

            pe.wait_ge(meta_ready, 1)
            for c in range(3):
                last = nc.tensor.matmul(bank[1][:, c * P:(c + 1) * P], win(arena, WIDE_AT + c * P, [[1, P]]), ident[:, :],
                                        start=True, stop=True)
            last.then_inc(meta_spread, 1)

            pe.wait_ge(tables_ready, 1)
            pe.wait_ge(early_in, 16)
            pe.wait_ge(late_in, 48)

            def xT(t, u):
                pe.wait_ge(t_loaded[u], (t // 4 + 1) * 16 if isinstance(t, int) else (t - u) * 4 + 16)
                if not (isinstance(t, int) and t < 2):
                    pe.wait_ge(t_xT_copied, t - 1)
                for k in range(KC):
                    last = nc.tensor.transpose(bank[u % 2][:, k * P:(k + 1) * P],
                                               win(work, u * ROW + k * P, [[1, P]]), ident[:, :])
                last.then_inc(t_xT, 1)

            def gate_up(t, u, e):
                pe.wait_ge(t_xT_copied, t + 1)
                if not (isinstance(t, int) and t < 2):
                    pe.wait_ge(t_h, t - 1)
                for k in range(KC):
                    last = nc.tensor.matmul(bank[2 + u % 2][:, 0:2 * M], win(work, XT_AT + u % 2 * L + k * P, [[1, P]]),
                                            wgu_v[:, bass.ds(e * WGU_E + k * 2 * M, 2 * M)],
                                            start=(k == 0), stop=(k == KC - 1))
                last.then_inc(t_gu, 1)

            def hT(t, u):
                pe.wait_ge(t_h, t + 1)
                if not (isinstance(t, int) and t < 2):
                    pe.wait_ge(t_hT_copied, t - 1)
                for c in range(2):
                    last = nc.tensor.transpose(bank[4 + u % 2][0:MH, c * P:(c + 1) * P],
                                               win(work, H_AT + u % 2 * M + c * MH, [[1, MH]]), ident[:, :])
                last.then_inc(t_hT, 1)

            def down(t, u, e):
                pe.wait_ge(t_hT_copied, t + 1)
                if not (isinstance(t, int) and t < 2):
                    pe.wait_ge(t_y_copied, t - 1)
                for c in range(2):
                    last = nc.tensor.matmul(bank[6 + u % 2][:, 0:L], win(work, HT_AT + u % 2 * L + c * P, [[1, P]], parts=MH),
                                            wd_v[:, bass.ds(e * WD_E + c * L, L)],
                                            start=(c == 0), stop=(c == 1))
                last.then_inc(t_y, 1)

            def expert(t):
                return pe.value_load(tile_exp[0:1, bass.ds(t, 1)], min_val=0, max_val=E - 1)

            def tile_step(t, u):
                if not isinstance(t, int) or t + 1 < NT:
                    xT(t + 1, (u + 1) % 4)
                if not isinstance(t, int) or t < NT:
                    gate_up(t, u, expert(t))
                if not isinstance(t, int) or 1 <= t <= NT:
                    hT(t - 1, (u + 3) % 4)
                if not isinstance(t, int) or t >= 2:
                    down(t - 2, (u + 2) % 4, expert(t - 2))

            xT(0, 0)
            for t in range(4):
                tile_step(t, t)
            with pe.Fori(1, NT // 4 - 1) as n:
                for u in range(4):
                    tile_step(n * 4 + u, u)
            for t in range(NT - 4, NT + 2):
                tile_step(t, t % 4)


def toeplitz_layout(kern):
    kern = np.asarray(kern)
    padded = np.concatenate([np.zeros((NH, P), kern.dtype), kern], axis=1)
    at = P + np.arange(L)[None, :] - np.arange(P)[:, None]
    return np.ascontiguousarray(padded[:, at].transpose(1, 0, 2)).reshape(P, NH * L)


def kernel(x, ctx_2048, g_xattn, g_ffn, L0_xattn_ssm_kernel, L0_xattn_D, L0_ffn_w_router,
           L0_ffn_corr_bias, L0_ffn_gate_w, L0_ffn_up_w, L0_ffn_down_w, L0_ffn_sh_gate_w,
           L0_ffn_sh_up_w, L0_ffn_sh_down_w):
    import concourse.bacc as bacc
    from concourse.bass_utils import run_bass_kernel_spmd

    c = np.asarray(ctx_2048).reshape(NG, GB, HD, BLK, P).transpose(0, 4, 3, 2, 1)
    gu = np.stack([np.asarray(L0_ffn_gate_w), np.asarray(L0_ffn_up_w)], axis=2)
    gu = gu.reshape(E, KC, P, 2 * M).transpose(2, 0, 1, 3)
    dn = np.asarray(L0_ffn_down_w).reshape(E, 2, MH, L).transpose(2, 0, 1, 3)
    arrays = {
        "x": np.asarray(x),
        "ctx_t": c.reshape(NG, P, BLK * HD * GB),
        "toeplitz": toeplitz_layout(L0_xattn_ssm_kernel),
        "g_xattn": np.asarray(g_xattn), "g_ffn": np.asarray(g_ffn),
        "skip_d": np.asarray(L0_xattn_D),
        "w_router": np.asarray(L0_ffn_w_router), "corr_bias": np.asarray(L0_ffn_corr_bias),
        "w_gu": gu.reshape(P, E * WGU_E), "w_down": dn.reshape(MH, E * WD_E),
        "sh_gu": np.stack([np.asarray(L0_ffn_sh_gate_w), np.asarray(L0_ffn_sh_up_w)]),
        "sh_down": np.asarray(L0_ffn_sh_down_w),
    }
    arrays = {n: np.ascontiguousarray(a) for n, a in arrays.items()}
    nc = bacc.Bacc("TRN2", target_bir_lowering=False, num_devices=1)
    args = [nc.dram_tensor(n, a.shape, mybir.dt.from_np(a.dtype), kind="ExternalInput").ap()
            for n, a in arrays.items()]
    out = nc.dram_tensor("out", (B, HD, L), mybir.dt.float32, kind="ExternalOutput").ap()
    build(nc, *args, out)
    return run_bass_kernel_spmd(nc, [arrays], core_ids=[0]).results[0]["out"]
```
